# Optimizing a Trainium2 kernel written in Bass

```python
import numpy as np
import jax
import jax.numpy as jnp

def _softmax(x, axis=-1):
    return jax.nn.softmax(x, axis=axis)

def _gelu(x):
    return jax.nn.gelu(x, approximate=True)

def _silu(x):
    return jax.nn.silu(x)

def _sigmoid(x):
    return jax.nn.sigmoid(x)

def _layernorm(x, axis=-1, eps=1e-05):
    m = jnp.mean(x, axis=axis, keepdims=True)
    v = jnp.var(x, axis=axis, keepdims=True)
    return (x - m) / jnp.sqrt(v + eps)

def _scatter_add(tgt, idx, src, axis=0):
    return tgt.at[idx].add(src)

def _segment_sum(src, seg, n):
    return jax.ops.segment_sum(src, seg, n)
kernel_name = 'mk_flamingo_gated_d2_seqx_r8_96afef'

def setup_inputs(seed: int=0):
    np.random.seed(seed)
    _w = jnp.asarray

    def _rec_inputs():
        import jax
        import jax.numpy as jnp
        _rk = jax.random.key(seed)
        x = -0.0002928 + 1 * jax.random.normal(jax.random.fold_in(_rk, 1), (4, 512, 128), jnp.float32)
        _lenS = 512 - jax.random.randint(jax.random.fold_in(_rk, 7), (4,), 0, max(1, 512 // 4) + 1, jnp.int32)
        _lenS2 = 154 - jax.random.randint(jax.random.fold_in(_rk, 8), (4,), 0, max(1, 154 // 4) + 1, jnp.int32)
        _ctx_1024P = jax.random.normal(jax.random.fold_in(_rk, 11), (4, 16, 128), jnp.float32)
        _ctx_1024c = jax.random.dirichlet(jax.random.fold_in(_rk, 511), 0.3 * jnp.ones((16,), jnp.float32), (4, 154))
        _ctx_1024t = jnp.einsum('bsk,bkd->bsd', _ctx_1024c, _ctx_1024P)
        _ctx_1024t = _ctx_1024t * jax.lax.rsqrt(jnp.mean(jnp.square(_ctx_1024t)) + 1e-12) * 0.953939
        ctx_1024 = -1.39393e-06 + 0.999914 * (_ctx_1024t + 0.3 * jax.random.normal(jax.random.fold_in(_rk, 611), (4, 154, 128), jnp.float32))
        _g = jax.random.normal(jax.random.fold_in(_rk, 9001), (2, 2), jnp.float32)
        _g = jnp.sign(_g) * jnp.maximum(jnp.abs(_g), 1.0) + (_g == 0) * 1.0
        g_xattn = _g[0]
        g_ffn = _g[1]
        return (x, ctx_1024, g_xattn, g_ffn)
    x, ctx_1024, g_xattn, g_ffn = _rec_inputs()

    def _L0_xattn_setup():
        import jax, jax.numpy as jnp
        import numpy as np
        DIM = 128
        NUM_HEADS = 16
        HEAD_DIM = DIM // NUM_HEADS
        key = jax.random.key(seed)
        ks = jax.random.split(key, 11)
        B, N, C = (2, 256, DIM)
        s = 1.0 / np.sqrt(C)
        inp = {'q': jax.random.normal(ks[0], (B, N, C), jnp.float32), 'k': jax.random.normal(ks[1], (B, N, C), jnp.float32), 'v': jax.random.normal(ks[2], (B, N, C), jnp.float32), 'Wq': jax.random.normal(ks[3], (C, C), jnp.float32) * s, 'bq': jnp.zeros((C,), jnp.float32), 'Wk': jax.random.normal(ks[4], (C, C), jnp.float32) * s, 'bk': jnp.zeros((C,), jnp.float32), 'Wv': jax.random.normal(ks[5], (C, C), jnp.float32) * s, 'bv': jnp.zeros((C,), jnp.float32), 'Wo': jax.random.normal(ks[6], (C, C), jnp.float32) * s, 'bo': jnp.zeros((C,), jnp.float32)}
        return inp
    _L0_xattn_all = _L0_xattn_setup()
    _L0_xattn_in = {k: v for k, v in _L0_xattn_all.items() if k in ('Wq', 'bq', 'Wk', 'bk', 'Wv', 'bv', 'Wo', 'bo')}
    del _L0_xattn_all

    def _L0_ffn_setup():
        import jax, jax.numpy as jnp
        import numpy as np
        BLOCK = 32
        W_BITS = 4
        ACT_BITS = 16

        def act_qdq(x):
            qmax = 2.0 ** (ACT_BITS - 1) - 1.0
            scale = jnp.maximum(jnp.max(jnp.abs(x)) / qmax, 1e-12)
            return jnp.clip(jnp.round(x / scale), -qmax - 1.0, qmax) * scale

        def fixed_qdq_u16(x):
            scale = 1.0 / 65536.0
            return jnp.clip(jnp.round(x / scale), 0.0, 65535.0) * scale

        def lpbq_dequant(w):
            O, I = w.shape
            qmax = 2.0 ** (W_BITS - 1) - 1.0
            wb = w.reshape(O, I // BLOCK, BLOCK)
            s = jnp.maximum(jnp.max(jnp.abs(wb), axis=-1, keepdims=True) / qmax, 1e-12)
            wq = jnp.clip(jnp.round(wb / s), -qmax - 1.0, qmax) * s
            return wq.reshape(O, I)
        key = jax.random.key(seed)
        k1, k2, k3, k4 = jax.random.split(key, 4)
        B, S, H, I = (2, 512, 128, 384)
        x = jax.random.normal(k1, (B, S, H), jnp.float32)
        w_gate = jax.random.normal(k2, (I, H), jnp.float32) * 0.02
        w_up = jax.random.normal(k3, (I, H), jnp.float32) * 0.02
        w_down = jax.random.normal(k4, (H, I), jnp.float32) * 0.02
        return {'x': x, 'w_gate': w_gate, 'w_up': w_up, 'w_down': w_down}
    _L0_ffn_all = _L0_ffn_setup()
    _L0_ffn_in = {k: v for k, v in _L0_ffn_all.items() if k in ('w_gate', 'w_up', 'w_down')}
    del _L0_ffn_all

    def _L1_xattn_setup():
        import jax, jax.numpy as jnp
        import numpy as np
        EMBED_DIM = 128
        NUM_HEADS = 16
        HEAD_DIM = EMBED_DIM // NUM_HEADS
        key = jax.random.key(seed)
        ks = jax.random.split(key, 11)
        s = 1.0 / np.sqrt(EMBED_DIM)
        inp = {'query': jax.random.normal(ks[0], (4, 256, EMBED_DIM), jnp.float32), 'key': jax.random.normal(ks[1], (4, 256, EMBED_DIM), jnp.float32), 'value': jax.random.normal(ks[2], (4, 256, EMBED_DIM), jnp.float32), 'Wq': jax.random.uniform(ks[3], (EMBED_DIM, EMBED_DIM), jnp.float32, -s, s), 'bq': jax.random.uniform(ks[4], (EMBED_DIM,), jnp.float32, -s, s), 'Wk': jax.random.uniform(ks[5], (EMBED_DIM, EMBED_DIM), jnp.float32, -s, s), 'bk': jax.random.uniform(ks[6], (EMBED_DIM,), jnp.float32, -s, s), 'Wv': jax.random.uniform(ks[7], (EMBED_DIM, EMBED_DIM), jnp.float32, -s, s), 'bv': jax.random.uniform(ks[8], (EMBED_DIM,), jnp.float32, -s, s), 'Wo': jax.random.uniform(ks[9], (EMBED_DIM, EMBED_DIM), jnp.float32, -s, s), 'bo': jax.random.uniform(ks[10], (EMBED_DIM,), jnp.float32, -s, s)}
        return inp
    _L1_xattn_all = _L1_xattn_setup()
    _L1_xattn_in = {k: v for k, v in _L1_xattn_all.items() if k in ('Wq', 'bq', 'Wk', 'bk', 'Wv', 'bv', 'Wo', 'bo')}
    del _L1_xattn_all

    def _L1_ffn_setup():
        import jax, jax.numpy as jnp
        import numpy as np
        from jax import lax
        T, B, I, M, O = (32, 64, 128, 128, 128)

        def _xavier(key, shape):
            fan_out, fan_in = shape
            limit = float(np.sqrt(6.0 / (fan_in + fan_out)))
            return jax.random.uniform(key, shape, jnp.float32, -limit, limit)
        key = jax.random.key(seed)
        ks = jax.random.split(key, 9)
        x = jax.random.normal(ks[0], (T, B, I), jnp.float32)
        return {'x': x, 'wf': _xavier(ks[1], (M, I)), 'uf': _xavier(ks[2], (M, M)), 'bf': jnp.zeros((M,), jnp.float32), 'wi': _xavier(ks[3], (M, I)), 'ui': _xavier(ks[4], (M, M)), 'bi': jnp.zeros((M,), jnp.float32), 'wc': _xavier(ks[5], (M, I)), 'uc': _xavier(ks[6], (M, M)), 'bc': jnp.zeros((M,), jnp.float32), 'wo': _xavier(ks[7], (O, I)), 'uo': _xavier(ks[8], (O, M)), 'bo': jnp.zeros((O,), jnp.float32), 'in_c': jnp.zeros((M,), jnp.float32)}
    _L1_ffn_all = _L1_ffn_setup()
    _L1_ffn_in = {k: v for k, v in _L1_ffn_all.items() if k in ('wf', 'uf', 'bf', 'wi', 'ui', 'bi', 'wc', 'uc', 'bc', 'wo', 'uo', 'bo', 'in_c')}
    del _L1_ffn_all
    return {'x': x, 'ctx_1024': ctx_1024, 'g_xattn': g_xattn, 'g_ffn': g_ffn, 'L0_xattn_Wq': _L0_xattn_in['Wq'], 'L0_xattn_bq': _L0_xattn_in['bq'], 'L0_xattn_Wk': _L0_xattn_in['Wk'], 'L0_xattn_bk': _L0_xattn_in['bk'], 'L0_xattn_Wv': _L0_xattn_in['Wv'], 'L0_xattn_bv': _L0_xattn_in['bv'], 'L0_xattn_Wo': _L0_xattn_in['Wo'], 'L0_xattn_bo': _L0_xattn_in['bo'], 'L0_ffn_w_gate': _L0_ffn_in['w_gate'], 'L0_ffn_w_up': _L0_ffn_in['w_up'], 'L0_ffn_w_down': _L0_ffn_in['w_down'], 'L1_xattn_Wq': _L1_xattn_in['Wq'], 'L1_xattn_bq': _L1_xattn_in['bq'], 'L1_xattn_Wk': _L1_xattn_in['Wk'], 'L1_xattn_bk': _L1_xattn_in['bk'], 'L1_xattn_Wv': _L1_xattn_in['Wv'], 'L1_xattn_bv': _L1_xattn_in['bv'], 'L1_xattn_Wo': _L1_xattn_in['Wo'], 'L1_xattn_bo': _L1_xattn_in['bo'], 'L1_ffn_wf': _L1_ffn_in['wf'], 'L1_ffn_uf': _L1_ffn_in['uf'], 'L1_ffn_bf': _L1_ffn_in['bf'], 'L1_ffn_wi': _L1_ffn_in['wi'], 'L1_ffn_ui': _L1_ffn_in['ui'], 'L1_ffn_bi': _L1_ffn_in['bi'], 'L1_ffn_wc': _L1_ffn_in['wc'], 'L1_ffn_uc': _L1_ffn_in['uc'], 'L1_ffn_bc': _L1_ffn_in['bc'], 'L1_ffn_wo': _L1_ffn_in['wo'], 'L1_ffn_uo': _L1_ffn_in['uo'], 'L1_ffn_bo': _L1_ffn_in['bo'], 'L1_ffn_in_c': _L1_ffn_in['in_c']}

def reference(x, ctx_1024, g_xattn, g_ffn, L0_xattn_Wq, L0_xattn_bq, L0_xattn_Wk, L0_xattn_bk, L0_xattn_Wv, L0_xattn_bv, L0_xattn_Wo, L0_xattn_bo, L0_ffn_w_gate, L0_ffn_w_up, L0_ffn_w_down, L1_xattn_Wq, L1_xattn_bq, L1_xattn_Wk, L1_xattn_bk, L1_xattn_Wv, L1_xattn_bv, L1_xattn_Wo, L1_xattn_bo, L1_ffn_wf, L1_ffn_uf, L1_ffn_bf, L1_ffn_wi, L1_ffn_ui, L1_ffn_bi, L1_ffn_wc, L1_ffn_uc, L1_ffn_bc, L1_ffn_wo, L1_ffn_uo, L1_ffn_bo, L1_ffn_in_c):
    import jax
    import jax.numpy as jnp

    def _L0_xattn_ref(q, k, v, Wq, bq, Wk, bk, Wv, bv, Wo, bo):
        import jax, jax.numpy as jnp
        import numpy as np
        DIM = 128
        NUM_HEADS = 16
        HEAD_DIM = DIM // NUM_HEADS
        B, Nq, C = q.shape
        Nkv = k.shape[1]
        H, D = (NUM_HEADS, HEAD_DIM)
        qh = (q @ Wq.T + bq).reshape(B, Nq, H, D).transpose(0, 2, 1, 3)
        kh = (k @ Wk.T + bk).reshape(B, Nkv, H, D).transpose(0, 2, 1, 3)
        vh = (v @ Wv.T + bv).reshape(B, Nkv, H, D).transpose(0, 2, 1, 3)
        scale = D ** (-0.5)
        attn = jax.nn.softmax(jnp.einsum('bhqd,bhkd->bhqk', qh, kh) * scale, axis=-1)
        out = jnp.einsum('bhqk,bhkd->bhqd', attn, vh)
        out = out.transpose(0, 2, 1, 3).reshape(B, Nq, C)
        return out @ Wo.T + bo

    def _L0_ffn_ref(x, w_gate, w_up, w_down):
        import jax, jax.numpy as jnp
        import numpy as np
        BLOCK = 32
        W_BITS = 4
        ACT_BITS = 16

        def act_qdq(x):
            qmax = 2.0 ** (ACT_BITS - 1) - 1.0
            scale = jnp.maximum(jnp.max(jnp.abs(x)) / qmax, 1e-12)
            return jnp.clip(jnp.round(x / scale), -qmax - 1.0, qmax) * scale

        def fixed_qdq_u16(x):
            scale = 1.0 / 65536.0
            return jnp.clip(jnp.round(x / scale), 0.0, 65535.0) * scale

        def lpbq_dequant(w):
            O, I = w.shape
            qmax = 2.0 ** (W_BITS - 1) - 1.0
            wb = w.reshape(O, I // BLOCK, BLOCK)
            s = jnp.maximum(jnp.max(jnp.abs(wb), axis=-1, keepdims=True) / qmax, 1e-12)
            wq = jnp.clip(jnp.round(wb / s), -qmax - 1.0, qmax) * s
            return wq.reshape(O, I)
        x = act_qdq(x)
        up = act_qdq(x @ lpbq_dequant(w_up).T)
        gate = act_qdq(x @ lpbq_dequant(w_gate).T)
        sig = fixed_qdq_u16(jax.nn.sigmoid(gate))
        gate = act_qdq(gate * sig)
        o = act_qdq(gate * up)
        return o @ lpbq_dequant(w_down).T

    def _L1_xattn_ref(query, key, value, Wq, bq, Wk, bk, Wv, bv, Wo, bo):
        import jax, jax.numpy as jnp
        import numpy as np
        EMBED_DIM = 128
        NUM_HEADS = 16
        HEAD_DIM = EMBED_DIM // NUM_HEADS
        B, T, E = query.shape
        S = key.shape[1]
        H, D = (NUM_HEADS, HEAD_DIM)
        q = (query @ Wq.T + bq).reshape(B, T, H, D).transpose(0, 2, 1, 3)
        k = (key @ Wk.T + bk).reshape(B, S, H, D).transpose(0, 2, 1, 3)
        v = (value @ Wv.T + bv).reshape(B, S, H, D).transpose(0, 2, 1, 3)
        scores = jnp.einsum('bhtd,bhsd->bhts', q, k) / np.sqrt(D)
        causal = jnp.triu(jnp.full((T, S), -jnp.inf, jnp.float32), k=1)
        scores = scores + causal[None, None]
        attn = jax.nn.softmax(scores, axis=-1)
        out = jnp.einsum('bhts,bhsd->bhtd', attn, v)
        out = out.transpose(0, 2, 1, 3).reshape(B, T, E)
        out = out @ Wo.T + bo
        return out

    def _L1_ffn_ref(x, wf, uf, bf, wi, ui, bi, wc, uc, bc, wo, uo, bo, in_c):
        import jax, jax.numpy as jnp
        import numpy as np
        from jax import lax
        T, B, I, M, O = (32, 64, 128, 128, 128)

        def _xavier(key, shape):
            fan_out, fan_in = shape
            limit = float(np.sqrt(6.0 / (fan_in + fan_out)))
            return jax.random.uniform(key, shape, jnp.float32, -limit, limit)
        batch = x.shape[1]
        c0 = jnp.broadcast_to(in_c, (batch, in_c.shape[0]))

        def step(c, xt):
            ft = jax.nn.sigmoid(xt @ wf.T + c @ uf.T + bf)
            it = jax.nn.sigmoid(xt @ wi.T + c @ ui.T + bi)
            gt = jnp.tanh(xt @ wc.T + c @ uc.T + bc)
            c = ft * c + it * gt
            return (c, None)
        c_final, _ = lax.scan(step, c0, x)
        h = jnp.tanh(jnp.einsum('tbi,oi->tbo', x, wo) + c_final @ uo.T + bo)
        return h
    x = x + jnp.tanh(g_xattn[0]) * _L0_xattn_ref(_layernorm(x, axis=-1), ctx_1024, ctx_1024, L0_xattn_Wq, L0_xattn_bq, L0_xattn_Wk, L0_xattn_bk, L0_xattn_Wv, L0_xattn_bv, L0_xattn_Wo, L0_xattn_bo)
    x = x + jnp.tanh(g_ffn[0]) * _L0_ffn_ref(_layernorm(x, axis=-1), L0_ffn_w_gate, L0_ffn_w_up, L0_ffn_w_down)
    x = x + jnp.tanh(g_xattn[1]) * _L1_xattn_ref(_layernorm(x, axis=-1), ctx_1024, ctx_1024, L1_xattn_Wq, L1_xattn_bq, L1_xattn_Wk, L1_xattn_bk, L1_xattn_Wv, L1_xattn_bv, L1_xattn_Wo, L1_xattn_bo)
    x = x + jnp.tanh(g_ffn[1]) * _L1_ffn_ref(_layernorm(x, axis=-1), L1_ffn_wf, L1_ffn_uf, L1_ffn_bf, L1_ffn_wi, L1_ffn_ui, L1_ffn_bi, L1_ffn_wc, L1_ffn_uc, L1_ffn_bc, L1_ffn_wo, L1_ffn_uo, L1_ffn_bo, L1_ffn_in_c)
    return x

_drawn_inputs = setup_inputs


def setup_inputs(seed=0):
    import zlib

    import numpy as np

    out = dict(_drawn_inputs(seed))
    spreads = {'g_ffn': (-1.0, 0.6),
     'L0_xattn_bq': (0.0, 0.434),
     'L0_xattn_bk': (0.0, 2.0),
     'L0_xattn_bv': (0.0, 0.1),
     'L0_xattn_bo': (0.0, 0.1),
     'L1_ffn_bf': (0.0, 2.0),
     'L1_ffn_bi': (0.0, 2.0),
     'L1_ffn_bc': (0.0, 0.783),
     'L1_ffn_bo': (0.0, 0.664),
     'L1_ffn_in_c': (0.0, 1.68)}
    factors = {'L0_ffn_w_gate': 7.368,
     'L0_ffn_w_up': 7.041,
     'L0_ffn_w_down': 7.063,
     'L1_xattn_Wq': 2.896,
     'L1_xattn_bq': 31.527,
     'L1_xattn_Wk': 2.739,
     'L1_xattn_bk': 200.0,
     'L1_xattn_bv': 7.149,
     'L1_xattn_bo': 4.228,
     'L1_ffn_wf': 3.224,
     'L1_ffn_uf': 4.917,
     'L1_ffn_ui': 4.634,
     'L1_ffn_wi': 2.687}
    for name, (base, spread) in spreads.items():
        noise = np.random.default_rng([zlib.crc32(name.encode()), seed]).standard_normal(out[name].shape)
        drawn = base * np.exp(spread * noise) if base else spread * noise
        out[name] = jnp.asarray(drawn.astype(out[name].dtype))
    for name, factor in factors.items():
        out[name] = (out[name] * factor).astype(out[name].dtype)
    return out
```

```python
from contextlib import ExitStack

import numpy as np

import concourse.bass as bass
from concourse import mybir

F32 = mybir.dt.float32
F32R = mybir.dt.float32r
I16 = mybir.dt.int16
U16 = mybir.dt.uint16
ALU = mybir.AluOpType
ACT = mybir.ActivationFunctionType
AX = mybir.AxisListType

P = 128
B, T, C = 4, 512, 128
TT = T // P
S = 154
H, D = 16, 8
G, J = 4, 4
NF = 3
TAIL0 = S - 32
OWN = P - TAIL0
SCALE = float(D) ** -0.5
EPS = 1e-5
NEG = -2.0 ** 126
QMAX = 32767.0
WMAX = 7.0
SMIN = 1e-12
NBLK = 36

KQ = 3 * D
KM = KQ + 2

SLOTS = 24
TILES = H + G
ROUNDS = 6
TOP0, TOP1 = 2, 16
PRING = 8
SRING = 3
MRING = 2
FRING = 7
PV_SLOT = {5: [0], 9: [1], 13: [2], 17: [3], 22: [4], 23: [5]}

WQ, WK, WV, WO = 0, 1, 2, 3
WL1 = 4
WF, UF, WI, UI, WC, UC, WOUT, UOUT = range(8, 16)
NW = 16
BQ, BK, BF, BI, BC, INC = 0, 2, 4, 5, 6, 7
RV, RO, RFO, RG = 0, 2, 4, 5


def max_units(layer):
    units = []
    for qt in range(TT):
        heads, keys = (G, P) if layer == 1 and qt == 0 else (G // 2, S)
        units += [(qt, h, heads, keys) for h in range(0, H, heads)]
    return units


UNITS = [max_units(0), max_units(1)]


def units_at(layer, slot):
    if not TOP0 <= slot < TOP1:
        return []
    n = len(UNITS[layer])
    return range(n * (slot - TOP0) // (TOP1 - TOP0), n * (slot - TOP0 + 1) // (TOP1 - TOP0))


def units_before(n):
    return sum(len(UNITS[m // B]) for m in range(n))


EVENTS = {3: ("wo", -1), 7: ("post", -1), 9: ("pre", 2), 11: ("q", 2), 17: ("top", 1)}


def events(i, slot):
    if slot in EVENTS and 0 <= i + EVENTS[slot][1] < B:
        yield EVENTS[slot][0], i + EVENTS[slot][1]


def norm_order():
    order = []
    for layer in range(2):
        for i in range(-2, B + 1):
            order += [(kind, layer, b) for kind, b in (("post", i - 1), ("pre", i + 2)) if 0 <= b < B]
    return order


NORMS = norm_order()
norm_no = {name: k for k, name in enumerate(NORMS)}


def misc_plan():
    order = [("k", 0, 0), ("k", 0, 1), ("v", 0), ("vt", 0)]
    for layer in range(2):
        for i in range(-2, B + 1):
            for slot in range(SLOTS):
                for name, b in events(i, slot):
                    order.append((name, layer, b))
                    if name == "post" and layer == 1:
                        order += [("gate", b, k) for k in range(3)]
            if layer == 0 and i == -1:
                order += [("k", 1, 0), ("k", 1, 1), ("v", 1), ("vt", 1), ("w", 0), ("w", 1), ("w", 2)]
        if layer == 0:
            order += [(kind, k) for k in range(5) for kind in ("gt", "gb")]
    return order


def program(nc, x, w, ctxT, tailT, wffn, cols, rows, consts, out):
    with ExitStack() as ctx:
        def sb(name, shape, dt=F32):
            return ctx.enter_context(nc.sbuf_tensor("sb_" + name, shape, dt))

        def bank(name):
            return ctx.enter_context(nc.psum_tensor("ps_" + name, [P, 512], F32))

        def sem(name):
            return ctx.enter_context(nc.semaphore(name))

        xr = sb("xr", [P, B * TT, C])
        wsb = sb("wsb", [P, NW, C])
        ctx_sb = sb("ctx", [P, B, S])
        tail_sb = sb("tail", [P, B, P])
        wf_sb = sb("wf", [P, NBLK, 32])
        wn16 = sb("wn16", [P, NBLK, 32], I16)
        wabs = sb("wabs", [P, 3, NBLK])
        wfT = sb("wfT", [P, 9, C])
        cols_sb = sb("cols", [P, 8])
        hcols = sb("hcols", [P, 8])
        rows_sb = sb("rows", [P, 6, C])
        tg = sb("tg", [P, 4])
        bog = sb("bog", [P, 2, C])
        bvt = sb("bvt", [P, 2, C])
        consts_sb = sb("consts", [P, 3 * P + 33])
        ident = consts_sb[:, 0:P]
        cmask = consts_sb[:, P:3 * P + 32]
        own = consts_sb[:, 3 * P + 32:3 * P + 33]
        identr = sb("identr", [P, P], F32R)
        maskr = sb("maskr", [P, 2 * P + 32], F32R)
        maskM, maskT, maskE = maskr[:, 0:P], maskr[:, P:2 * P], maskr[:, 2 * P:2 * P + 32]
        ones = sb("ones", [P, P])
        stat6 = sb("stat6", [P, 4, TT, 6])
        mv = sb("mv", [P, 4, TT, 2])
        var = sb("var", [P, 4, TT])
        half = sb("half", [P, TT])
        rstd = sb("rstd", [P, 4, TT])
        xn = sb("xn", [P, 2, TT, C])
        pnT = sb("pnT", [P, B, T])
        Q4 = [sb(f"Q4{n}", [P, G, T], F32R) for n in range(3)]
        K4_1 = sb("K41", [P, G, B, S], F32R)
        KT_1 = sb("KT1", [P, B, G, P], F32R)
        V4_1 = sb("V41", [P, B, G, J, 32])
        VT_1 = sb("VT1", [P, B, G, 64])
        nm = sb("nm", [P, TT, H])
        nms = sb("nms", [P, TT, J, 2, G], F32R)
        orc = sb("orc", [P, 2, T // 32, 2])
        amax = sb("amax", [P, 5, 12])
        amx = sb("amx", [P, 5])
        gtop = sb("gtop", [1, 5])
        sc = sb("sc", [P, 5, 4])
        cst = sb("cst", [P, T])

        with ExitStack() as stretch:
            def sb_here(name, shape, dt=F32):
                return stretch.enter_context(nc.sbuf_tensor("sb_" + name, shape, dt))

            xg = sb_here("xg", [P, 2, TT, C])
            kh = sb_here("kh", [P, B * S], F32R)
            kl = sb_here("kl", [P, B * S], F32R)
            qh = sb_here("qh", [P, 2, T], F32R)
            ql = sb_here("ql", [P, 2, T], F32R)
            nmT = sb_here("nmT", [32, 2, T], F32R)
            pr = sb_here("pr", [P, PRING, T])
            oq = sb_here("oq", [P, 2, T // 32, 2, 16])
            oc = sb_here("oc", [P, T // 32, 2, 2, D])
            oT = sb_here("oT", [P, T])
            gt = sb_here("gt", [P, 3, T])
            tmp = sb_here("tmp", [P, 2, T])
            yt = sb_here("yt", [P, B, TT, C])
            xnT = sb_here("xnT", [P, T])
            K4 = [sb_here("K40", [P, G, B, S], F32R), K4_1]
            KT = [sb_here("KT0", [P, B, G, P], F32R), KT_1]
            V4 = [sb_here("V40", [P, B, G, J, 32]), V4_1]
            VT = [sb_here("VT0", [P, B, G, 64]), VT_1]
        with ExitStack() as stretch:
            def sb_here(name, shape, dt=F32):
                return stretch.enter_context(nc.sbuf_tensor("sb_" + name, shape, dt))

            n16 = sb_here("n16", [P, B, T], I16)
            xq = sb_here("xq", [P, B, T])
            gf = sb_here("gf", [P, B, NF, T])
            uf = sb_here("uf", [P, B, NF, T])
            g16 = sb_here("g16", [P, B, NF, T], I16)
            s16 = sb_here("s16", [P, B, NF, T], U16)
            u16 = sb_here("u16", [P, B, NF, T], I16)

        score = [bank(f"score{n}") for n in range(SRING)]
        top = [bank(f"top{n}") for n in range(MRING)]
        pv = [bank(f"pv{n}") for n in range(2)]
        misc = bank("misc")
        fbank = score + top + pv

        x_in = [sem(f"x_in{b}") for b in range(B)]
        w_in, small_in, ctx_in, wl_in, wf_in = (sem(n) for n in ("w_in", "small_in", "ctx_in", "wl_in", "wf_in"))
        const_r = sem("const_r")
        gates = sem("gates")
        hcol_r = sem("hcol_r")
        bias_r = sem("bias_r")
        ones_r, half_r = sem("ones_r"), sem("half_r")
        zero_r = sem("zero_r")
        misc_full = sem("misc_full")
        kh_r, kl_r = sem("kh_r"), sem("kl_r")
        k_in = [sem(f"k_in{n}") for n in range(2)]
        kt_r = sem("kt_r")
        v_r, vread_r = sem("v_r"), sem("vread_r")
        stats_r, mv_r, var_r, rstd_r, xn_r, xnT_r = (sem(n) for n in ("stats_r", "mv_r", "var_r", "rstd_r", "xn_r", "xnT_r"))
        qh_r, ql_r = sem("qh_r"), sem("ql_r")
        q_in = [sem(f"q_in{n}") for n in range(3)]
        m_in = [sem(f"m_in{n}") for n in range(3)]
        top_r, top_red = sem("top_r"), sem("top_red")
        nmh_r, nms_r, nmT_r = sem("nmh_r"), sem("nms_r"), sem("nmT_r")
        score_r, exp_r, pv_r = sem("score_r"), sem("exp_r"), sem("pv_r")
        pvx = sem("pvx")
        orc_r, oc_r, oT_r = sem("orc_r"), sem("oc_r"), sem("oT_r")
        xg_r, res_r = sem("xg_r"), sem("res_r")
        wq_r, wT_r = sem("wq_r"), sem("wT_r")
        fmm, fev = sem("fmm"), sem("fev")
        am_r, amx_r, gtop_r, sc_r = sem("am_r"), sem("amx_r"), sem("gtop_r"), sem("sc_r")
        xq_r, g16_r, th_r, s16_r, g2_r, n2_r, u16_r, o_r, n3_r, xo_r = (
            sem(n) for n in ("xq_r", "g16_r", "th_r", "s16_r", "g2_r", "n2_r", "u16_r", "o_r", "n3_r", "xo_r"))
        n16_r, smax_r = sem("n16_r"), sem("smax_r")
        dmm, x2_r = sem("dmm"), sem("x2_r")
        gt_r, ct_r, c_r = sem("gt_r"), sem("ct_r"), sem("c_r")
        ymm, y_r, out_r, out_in = sem("ymm"), sem("y_r"), sem("out_r"), sem("out_in")

        misc_uses = misc_plan()
        use = {name: n for n, name in enumerate(misc_uses)}

        def misc_read(name):
            kind = name[0]
            if kind == "k":
                return kl_r, 2 * name[1] + name[2] + 1
            if kind in ("v", "vt"):
                return vread_r, 2 * name[1] + (kind == "vt") + 1
            if kind in ("pre", "post"):
                return xnT_r, norm_no[name] + 1
            if kind == "q":
                return ql_r, B * name[1] + name[2] + 1
            if kind == "top":
                return nmT_r, B * name[1] + name[2] + 1
            if kind == "wo":
                return res_r, B * name[1] + name[2] + 1
            if kind == "gate":
                return gt_r, 3 * name[1] + name[2] + 1
            if kind == "w":
                return wT_r, name[1] + 1
            return (gtop_r if kind == "gt" else smax_r), name[1] + 1

        block = ctx.enter_context(nc.Block())

        def fill_misc(pe, name):
            if use[name] > 0:
                pe.wait_ge(*misc_read(misc_uses[use[name] - 1]))

        def weight(n):
            return wsb[:, n, :]

        def head(k):
            return k % G, k // G

        @block.sync
        def _(sp):
            xd = x.rearrange("b (t p) c -> p b t c", p=P)
            sp.dma_start(xr[:, 0:TT, :], xd[:, 0]).then_inc(x_in[0], 16)
            sp.dma_start(wsb[:, 0:4, :], w[:, 0:4, :]).then_inc(w_in, 16)
            sp.dma_start(ctx_sb[:, :, :], ctxT).then_inc(ctx_in, 16)
            sp.dma_start(tail_sb[:, :, :], tailT).then_inc(ctx_in, 16)
            for b in range(1, B):
                sp.dma_start(xr[:, TT * b:TT * b + TT, :], xd[:, b]).then_inc(x_in[b], 16)
            sp.dma_start(wf_sb[:, :, :], wffn).then_inc(wf_in, 16)
            sp.dma_start(wsb[:, 4:NW, :], w[:, 4:NW, :]).then_inc(wl_in, 16)

            def keys(layer):
                sp.wait_ge(zero_r, 1 if layer == 0 else 8)
                for src, row in ((kh, 0), (kh, D), (kl, 2 * D)):
                    sp.wait_ge(kh_r if src is kh else kl_r, 2 * layer + 2)
                    for j in range(J):
                        sp.dma_start(K4[layer][32 * j + row:32 * j + row + D, :, :, :].bitcast(F32),
                                     src[32 * j:32 * j + 32, :].bitcast(F32)).then_inc(k_in[layer], 16)

            def queries(layer, b):
                n = B * layer + b
                sp.wait_ge(zero_r, 7)
                if n >= 3:
                    sp.wait_ge(score_r, TILES * (n - 2))
                for src, row in ((qh, 0), (ql, D), (qh, 2 * D)):
                    sp.wait_ge(qh_r if src is qh else ql_r, n + 1)
                    for j in range(J):
                        sp.dma_start(Q4[n % 3][32 * j + row:32 * j + row + D, :, :].bitcast(F32),
                                     src[32 * j:32 * j + 32, n % 2, :].bitcast(F32)).then_inc(q_in[n % 3], 16)

            def tops(layer, b):
                n = B * layer + b
                sp.wait_ge(nmT_r, n + 1)
                for j in range(J):
                    sp.dma_start(Q4[n % 3][32 * j + KQ:32 * j + KM, :, :].bitcast(F32),
                                 nmT[8 * j:8 * j + 8, n % 2, :].bitcast(F32)).then_inc(m_in[n % 3], 16)

            keys(0)
            for layer in range(2):
                for i in range(-2, B + 1):
                    for slot in range(SLOTS):
                        for name, b in events(i, slot):
                            if name == "q":
                                queries(layer, b)
                            if name == "top":
                                tops(layer, b)
                    if layer == 0 and i == -1:
                        keys(1)
            od = out.rearrange("b (t p) c -> p b t c", p=P)
            for b in range(B):
                sp.wait_ge(out_r, b + 1)
                sp.dma_start(od[:, b], yt[:, b, :, :]).then_inc(out_in, 16)
            sp.wait_ge(out_in, 16 * B)

        @block.gpsimd
        def _(pool):
            pool.memset(half[:, :], -0.5).then_inc(half_r, 1)

            def clear(layer):
                pool.memset(K4[layer][:, :, :, :].bitcast(F32), 1.0).then_inc(zero_r, 1)
                pool.memset(V4[layer][:, :, :, :, :], 0.0).then_inc(zero_r, 1)
                pool.memset(VT[layer][:, :, :, :], 0.0).then_inc(zero_r, 1)
                pool.memset(KT[layer][:, :, :, :].bitcast(F32), 0.0).then_inc(zero_r, 1)

            clear(0)
            for n in range(3):
                pool.memset(Q4[n][:, :, :].bitcast(F32), 0.0).then_inc(zero_r, 1)

            def biased(layer, b):
                n = B * layer + b
                if n >= 2:
                    pool.wait_ge(res_r, n - 1)
                if layer == 1:
                    pool.wait_ge(x2_r, b + 1)
                else:
                    pool.wait_ge(x_in[b], 16)
                pool.wait_ge(bias_r, 2)
                for t in range(TT):
                    ins = pool.tensor_tensor(xg[:, n % 2, t, :], xr[:, TT * b + t, :], bog[:, layer, :], ALU.add)
                ins.then_inc(xg_r, 1)

            def root(k):
                pool.wait_ge(mv_r, k + 1)
                pool.tensor_scalar(var[:, k % 4, :], mv[:, k % 4, :, 1], EPS, 1.0, ALU.add, ALU.mult).then_inc(var_r, 1)
                pool.wait_ge(var_r, k + 1)
                pool.tensor_tensor(rstd[:, k % 4, :], var[:, k % 4, :], half[:, :], ALU.pow).then_inc(rstd_r, 1)

            pool.wait_ge(half_r, 1)
            for kind, layer, b in NORMS:
                root(norm_no[kind, layer, b])
                if (kind, layer, b) == ("pre", 0, 0):
                    clear(1)
                if kind == "pre":
                    biased(layer, b)

        @block.scalar
        def _(act):
            act.dma_start(cols_sb[:, :], cols).then_inc(small_in, 16)
            act.dma_start(rows_sb[:, :, :], rows.partition_broadcast(P)).then_inc(small_in, 16)
            act.dma_start(consts_sb[:, :], consts).then_inc(small_in, 16)
            act.wait_ge(small_in, 48)
            act.activation(tg[:, :], rows_sb[:, RG, 0:4], ACT.Tanh).then_inc(gates, 1)
            act.activation(hcols[:, :], cols_sb[:, :], ACT.Copy, scale=0.5).then_inc(hcol_r, 1)
            act.activation(identr[:, :], ident[:, :], ACT.Copy).then_inc(const_r, 1)
            act.activation(maskr[:, :], cmask[:, :], ACT.Copy).then_inc(const_r, 1)

            def copy_k(layer):
                for part in range(2):
                    act.wait_ge(misc_full, use["k", layer, part] + 1)
                    if layer == 1:
                        act.wait_ge(k_in[0], 12 * 16)
                    act.activation(kh[:, 308 * part:308 * part + 308], misc[:, 0:308], ACT.Identity,
                                   bias=cols_sb[:, BK + layer:BK + layer + 1]).then_inc(kh_r, 1)

            def copy_normed(kind, layer, b):
                act.wait_ge(misc_full, use[kind, layer, b] + 1)
                if kind == "pre":
                    if (layer, b) != (0, 0):
                        act.wait_ge(qh_r, B * layer + b)
                    dst = xnT[:, :]
                else:
                    dst = pnT[:, b, :]
                    if layer == 1:
                        act.wait_ge(n16_r, B)
                act.activation(dst, misc[:, :], ACT.Copy).then_inc(xnT_r, 1)

            def copy_q(layer, b):
                n = B * layer + b
                act.wait_ge(misc_full, use["q", layer, b] + 1)
                if n >= 2:
                    act.wait_ge(q_in[(n - 2) % 3], 12 * 16 * ((n - 2) // 3 + 1))
                act.activation(qh[:, n % 2, :], misc[:, :], ACT.Identity,
                               bias=cols_sb[:, BQ + layer:BQ + layer + 1]).then_inc(qh_r, 1)

            def copy_top(layer, b):
                n = B * layer + b
                act.wait_ge(misc_full, use["top", layer, b] + 1)
                if n >= 2:
                    act.wait_ge(m_in[(n - 2) % 3], 4 * 16 * ((n - 2) // 3 + 1))
                act.activation(nmT[:, n % 2, :], misc[0:32, :], ACT.Copy).then_inc(nmT_r, 1)

            def exps(layer, b, t):
                k = TILES * (B * layer + b) + t
                act.wait_ge(score_r, k + 1)
                if k >= PRING:
                    m, old = divmod(k - PRING, TILES)
                    act.wait_ge(pv_r, ROUNDS * m + (old // 4 + 1 if old < H else ROUNDS))
                q0 = P if layer == 1 and t >= H else 0
                act.activation(pr[:, k % PRING, q0:T], score[k % SRING][:, q0:T], ACT.Exp, scale=SCALE).then_inc(exp_r, 1)

            def gates_of(b):
                for k, col, s in ((0, BF, 0.5), (1, BI, 0.5), (2, BC, 1.0)):
                    act.wait_ge(misc_full, use["gate", b, k] + 1)
                    if b > 0:
                        act.wait_ge(c_r, b + 2)
                    bias = (hcols if s == 0.5 else cols_sb)[:, col:col + 1]
                    act.activation(gt[:, k, :], misc[:, :], ACT.Tanh, bias=bias, scale=s).then_inc(gt_r, 1)

            copy_k(0)
            for layer in range(2):
                for i in range(-2, B + 1):
                    for slot in range(SLOTS):
                        if 0 <= i < B and slot < TILES:
                            exps(layer, i, slot)
                        for name, b in events(i, slot):
                            if name in ("pre", "post"):
                                copy_normed(name, layer, b)
                            if name == "q":
                                copy_q(layer, b)
                            if name == "top":
                                copy_top(layer, b)
                            if name == "post" and layer == 1:
                                gates_of(b)
                    if layer == 0 and i == -1:
                        copy_k(1)
                        for k in range(3):
                            n = min(4, 9 - 4 * k)
                            act.wait_ge(misc_full, use["w", k] + 1)
                            act.activation(wfT[:, 4 * k:4 * k + n, :], misc[:, 0:n * P], ACT.Copy).then_inc(wT_r, 1)
                if layer == 0:
                    for t in range(24):
                        act.wait_ge(fmm, t + 1)
                        dst = gf if t < 12 else uf
                        act.activation(dst[:, t % 12 // 3, t % 3, :], fbank[t % FRING][:, :], ACT.Copy).then_inc(fev, 1)
                        if t >= 20:
                            c = t - 20
                            act.wait_ge(g16_r, c + 1)
                            act.wait_ge(sc_r, 2)
                            act.activation(gf[:, c, :, :], g16[:, c, :, :], ACT.Tanh, scale=sc[:, 1, 3:4]).then_inc(th_r, 1)
                    for c in range(B):
                        act.wait_ge(sc_r, 3)
                        act.activation(u16[:, c, :, :], uf[:, c, :, :], ACT.Copy, scale=sc[:, 2, 2:3]).then_inc(u16_r, 1)
                    for c in range(B):
                        act.wait_ge(n3_r, c + 1)
                        act.activation(gf[:, c, :, :], g16[:, c, :, :], ACT.Copy, scale=sc[:, 4, 1:2]).then_inc(xo_r, 1)
            for b in range(B):
                act.wait_ge(ymm, b + 1)
                act.activation(yt[:, b, :, :], fbank[b][:, :], ACT.Tanh).then_inc(y_r, 1)

        @block.tensor
        def _(pe):
            def keys_values(layer):
                wl = WL1 * layer
                for part in range(2):
                    fill_misc(pe, ("k", layer, part))
                    pe.matmul(misc[:, 0:308], weight(wl + WK), ctx_sb[:, 2 * part:2 * part + 2, :],
                              start=True, stop=True).then_inc(misc_full, 1)
                for kind in ("v", "vt"):
                    fill_misc(pe, (kind, layer))
                    for b in range(B):
                        keys = ctx_sb[:, b, 0:P] if kind == "v" else tail_sb[:, b, :]
                        ins = pe.matmul(misc[:, P * b:P * b + P], keys, weight(wl + WV), start=True, stop=True)
                    ins.then_inc(misc_full, 1)

            def turn_normed(kind, layer, b):
                k = norm_no[kind, layer, b]
                pe.wait_ge(xn_r, k + 1)
                fill_misc(pe, (kind, layer, b))
                for t in range(TT):
                    ins = pe.transpose(misc[:, P * t:P * t + P], xn[:, kind == "post", t, :], ident[:, :])
                ins.then_inc(misc_full, 1)

            def project_q(layer, b):
                pe.wait_ge(xnT_r, norm_no["pre", layer, b] + 1)
                fill_misc(pe, ("q", layer, b))
                pe.matmul(misc[:, :], weight(WL1 * layer + WQ), xnT[:, :], start=True, stop=True).then_inc(misc_full, 1)

            def scores_for_top(layer, b, u):
                n = B * layer + b
                k = units_before(n) + u
                if u == 0:
                    pe.wait_ge(q_in[n % 3], 12 * 16 * (n // 3 + 1))
                    if b == 0:
                        pe.wait_ge(k_in[layer], 12 * 16)
                if k >= MRING:
                    pe.wait_ge(top_red, k - MRING + 1)
                qt, h0, heads, keys = UNITS[layer][u]
                masked = layer == 1 and qt < 2
                ps = top[k % MRING]
                for m in range(heads):
                    g, j = head(h0 + m)
                    ins = pe.matmul(ps[:, keys * m:keys * m + keys],
                                    Q4[n % 3][32 * j:32 * j + KQ, g, P * qt:P * qt + P],
                                    K4[layer][32 * j:32 * j + KQ, g, b, 0:keys],
                                    start=(m == 0), stop=not masked, skip_group_check=True)
                if masked:
                    lo = 0 if qt == 0 else P
                    for m in range(heads):
                        ins = pe.matmul(ps[:, keys * m + lo:keys * m + keys], identr[:, :], maskM[:, 0:keys - lo],
                                        start=False, stop=True, skip_group_check=True)
                ins.then_inc(top_r, 1)

            def turn_top(layer, b):
                n = B * layer + b
                pe.wait_ge(nms_r, n + 1)
                fill_misc(pe, ("top", layer, b))
                for t in range(TT):
                    ins = pe.transpose(misc[0:32, P * t:P * t + P],
                                       nms[:, t, :, :, :].rearrange("p j a g -> p (j a g)").bitcast(F32), ident[:, :])
                ins.then_inc(misc_full, 1)

            def scores(layer, b, t):
                n = B * layer + b
                k = TILES * n + t
                if t == 0:
                    pe.wait_ge(m_in[n % 3], 4 * 16 * (n // 3 + 1))
                if k >= SRING:
                    pe.wait_ge(exp_r, k - SRING + 1)
                ps = score[k % SRING]
                if t < H:
                    g, j = t % G, t // G
                    ins = pe.matmul(ps[:, :], K4[layer][32 * j:32 * j + KM, g, b, 0:P],
                                    Q4[n % 3][32 * j:32 * j + KM, g, :], start=True, stop=(layer == 0),
                                    skip_group_check=True)
                    if layer == 1:
                        ins = pe.matmul(ps[:, 0:P], identr[:, :], maskT, start=False, stop=True, skip_group_check=True)
                else:
                    if t == H and b == 0:
                        pe.wait_ge(kt_r, 4 * layer + 4)
                    q0 = P if layer == 1 else 0
                    ins = pe.matmul(ps[:, q0:T], KT[layer][:, b, t - H, :], Q4[n % 3][:, t - H, q0:T],
                                    start=True, stop=(layer == 0), skip_group_check=True)
                    if layer == 1:
                        ins = pe.matmul(ps[:, P:P + 32], identr[:, :], maskE, start=False, stop=True,
                                        skip_group_check=True)
                ins.then_inc(score_r, 1)

            def weigh(layer, b, r):
                n = B * layer + b
                if r == 0 and b == 0:
                    pe.wait_ge(v_r, 8 * layer + 8)
                if r in (0, 2) and n > 0:
                    pe.wait_ge(pvx, 2 * (n - 1) + r // 2 + 1)
                pe.wait_ge(exp_r, TILES * n + (4 * r + 4 if r < 4 else TILES))
                acc = pv[r // 2 if r < 4 else r - 4]
                q0 = P if layer == 1 and r >= 4 else 0
                for g in range(G):
                    if r < 4:
                        lhs, t = V4[layer][:, b, g, r, :], 4 * r + g
                    else:
                        lhs, t = VT[layer][:, b, g, 32 * (r - 4):32 * (r - 4) + 32], H + g
                    ins = pe.matmul(acc[32 * g:32 * g + 32, q0:T], lhs, pr[:, (TILES * n + t) % PRING, q0:T],
                                    start=(r in (0, 2)), stop=(r >= 4), skip_group_check=True)
                ins.then_inc(pv_r, 1)

            def project_out(layer, b):
                n = B * layer + b
                pe.wait_ge(oT_r, n + 1)
                fill_misc(pe, ("wo", layer, b))
                for t in range(TT):
                    ins = pe.matmul(misc[:, P * t:P * t + P], oT[:, P * t:P * t + P], weight(WL1 * layer + WO),
                                    start=True, stop=True)
                ins.then_inc(misc_full, 1)

            def step(b):
                pe.wait_ge(xnT_r, norm_no["post", 1, b] + 1)
                pe.wait_ge(c_r, b + 2)
                for k, wx in enumerate((WF, WI, WC)):
                    fill_misc(pe, ("gate", b, k))
                    pe.matmul(misc[:, :], weight(wx), pnT[:, b, :], start=True, stop=False)
                    pe.matmul(misc[:, :], weight(wx + 1), cst[:, :], start=False, stop=True).then_inc(misc_full, 1)

            def global_top(k):
                pe.wait_ge(amx_r, k + 1)
                fill_misc(pe, ("gt", k))
                pe.transpose(misc[0:1, 0:P], amx[:, k:k + 1], ident[:, :]).then_inc(misc_full, 1)
                pe.wait_ge(gtop_r, k + 1)
                fill_misc(pe, ("gb", k))
                pe.matmul(misc[:, 0:1], ones[0:1, :], gtop[0:1, k:k + 1], start=True, stop=True).then_inc(misc_full, 1)

            pe.wait_ge(w_in, 16)
            pe.wait_ge(ctx_in, 32)
            keys_values(0)
            for layer in range(2):
                for i in range(-2, B + 1):
                    for slot in range(SLOTS):
                        if 0 <= i < B and slot < TILES:
                            scores(layer, i, slot)
                        if 0 <= i + 1 < B:
                            for u in units_at(layer, slot):
                                scores_for_top(layer, i + 1, u)
                        if 0 <= i < B:
                            for r in PV_SLOT.get(slot, []):
                                weigh(layer, i, r)
                        for name, b in events(i, slot):
                            if name in ("pre", "post"):
                                if (name, layer, b) == ("pre", 0, 0):
                                    pe.wait_ge(small_in, 48)
                                if (name, layer, b) == ("pre", 1, 0):
                                    pe.wait_ge(const_r, 2)
                                turn_normed(name, layer, b)
                            if name == "q":
                                project_q(layer, b)
                            if name == "top":
                                turn_top(layer, b)
                            if name == "wo":
                                project_out(layer, b)
                            if name == "post" and layer == 1:
                                step(b)
                    if layer == 0 and i == -1:
                        pe.wait_ge(wl_in, 16)
                        keys_values(1)
                        pe.wait_ge(wq_r, 1)
                        for k in range(3):
                            fill_misc(pe, ("w", k))
                            for m in range(4 * k, min(4 * k + 4, 9)):
                                blk = wf_sb[:, 4 * m:4 * m + 4, :].rearrange("p a c -> p (a c)")
                                ins = pe.transpose(misc[:, P * (m % 4):P * (m % 4) + P], blk, ident[:, :])
                            ins.then_inc(misc_full, 1)
                if layer == 0:
                    pe.wait_ge(ones_r, 1)
                    pe.wait_ge(wT_r, 3)
                    pe.wait_ge(pvx, 2 * B)
                    pe.wait_ge(exp_r, TILES * B)
                    pe.wait_ge(top_red, units_before(B))
                    global_top(0)
                    for t in range(24):
                        c, m = t % 12 // 3, t % 3
                        if t < 12 and m == 0:
                            pe.wait_ge(xq_r, c + 1)
                        if t >= FRING:
                            pe.wait_ge(fev, t - FRING + 1)
                        pe.matmul(fbank[t % FRING][:, :], wfT[:, 3 * (t // 12) + m, :], xq[:, c, :],
                                  start=True, stop=True).then_inc(fmm, 1)
                        if t == 16:
                            global_top(1)
                    for k in range(2, 5):
                        global_top(k)
                    for c in range(B):
                        pe.wait_ge(xo_r, c + 1)
                        if c == 0:
                            pe.wait_ge(fev, 24)
                        for t in range(TT):
                            for m in range(NF):
                                ins = pe.matmul(fbank[c][:, P * t:P * t + P], gf[:, c, m, P * t:P * t + P],
                                                wfT[:, 6 + m, :], start=(t == 0 and m == 0), stop=(m == NF - 1),
                                                skip_group_check=True)
                        ins.then_inc(dmm, 1)
                    pe.wait_ge(x2_r, B)
            pe.wait_ge(exp_r, 2 * TILES * B)
            pe.wait_ge(top_red, units_before(2 * B))
            for b in range(B):
                pe.matmul(fbank[b][:, :], ones[0:1, :], rows_sb[0:1, RFO:RFO + 1, :].to_broadcast([1, TT, C]),
                          start=True, stop=False, skip_group_check=True)
                for t in range(TT):
                    pe.matmul(fbank[b][:, P * t:P * t + P], pnT[:, b, P * t:P * t + P], weight(WOUT),
                              start=False, stop=False, skip_group_check=True)
            pe.wait_ge(c_r, B + 2)
            for b in range(B):
                for t in range(TT):
                    ins = pe.matmul(fbank[b][:, P * t:P * t + P], cst[:, P * t:P * t + P], weight(UOUT),
                                    start=False, stop=True, skip_group_check=True)
                ins.then_inc(ymm, 1)

        @block.vector
        def _(dve):
            chained = [0]
            chain = ctx.enter_context(nc.semaphore("chain"))

            def link(ins):
                chained[0] += 1
                ins.then_inc(chain, 1)
                dve.wait_ge(chain, chained[0])

            def values(layer):
                V, E = V4[layer], VT[layer]
                dve.wait_ge(zero_r, 3 if layer == 0 else 10)
                dve.wait_ge(misc_full, use["v", layer] + 1)
                pv4 = misc[:, :].rearrange("p (b g j d) -> p b g j d", b=B, g=G, j=J)
                bias = rows_sb[:, RV + layer, :].rearrange("p (g j d) -> p g j d", g=G, j=J)
                tbias = bvt[:, layer, :].rearrange("p (g j d) -> p g j d", g=G, j=J)
                for j in range(J):
                    c = 16 * (j % 2)
                    for b in range(B):
                        ins = dve.tensor_tensor(V[:, b, :, j, c:c + D], pv4[:, b, :, j, :], bias[:, :, j, :], ALU.add)
                    if j == J - 1:
                        ins.then_inc(vread_r, 1)
                    dve.memset(V[:, :, :, j, c + D:c + 2 * D], 1.0).then_inc(v_r, 1)
                dve.wait_ge(misc_full, use["vt", layer] + 1)
                for j in range(J):
                    q = slice(32 * j, 32 * j + 32)
                    for b in range(B):
                        ins = dve.tensor_tensor(E[q, b, :, 16 * j:16 * j + D], pv4[q, b, :, j, :], tbias[q, :, j, :], ALU.add)
                    if j == J - 1:
                        ins.then_inc(vread_r, 1)
                    on = ones[q, :].rearrange("p (b g d) -> p b g d", b=B, g=G)
                    dve.tensor_scalar(E[q, :, :, 16 * j + D:16 * j + 2 * D], on, own[q, 0:1], None, ALU.mult).then_inc(v_r, 1)

            def keys(layer):
                if layer == 1:
                    dve.wait_ge(k_in[0], 12 * 16)
                for part in range(2):
                    dve.wait_ge(kh_r, 2 * layer + part + 1)
                    cut = slice(308 * part, 308 * part + 308)
                    ins = dve.scalar_tensor_tensor(out=kl[:, cut], in0=misc[:, 0:308],
                                                   scalar=cols_sb[:, BK + layer:BK + layer + 1],
                                                   in1=kh[:, cut].bitcast(F32), op0=ALU.add, op1=ALU.subtract)
                    ins.then_inc(kl_r, 1)
    
            def tail_keys(layer):
                dve.wait_ge(k_in[layer], 12 * 16)
                dve.wait_ge(zero_r, 4 if layer == 0 else 11)
                for j in range(J):
                    q = slice(32 * j, 32 * j + 32)
                    dve.tensor_copy(KT[layer][q, :, :, 32 * j:32 * j + 32],
                                    K4[layer][q, :, :, TAIL0:S].bitcast(F32).rearrange("p g b s -> p b g s")).then_inc(kt_r, 1)

            def weights():
                dve.wait_ge(wf_in, 16)
                link(dve.tensor_reduce(wabs[:, 0, :], wf_sb[:, :, :], AX.X, ALU.max, apply_absolute_value=True))
                link(dve.tensor_scalar(wabs[:, 1, :], wabs[:, 0, :], 1.0 / WMAX, SMIN, ALU.mult, ALU.max))
                link(dve.reciprocal(wabs[:, 2, :], wabs[:, 1, :]))
                wide = [P, NBLK, 32]
                link(dve.tensor_tensor(wn16[:, :, :], wf_sb[:, :, :],
                                       wabs[:, 2, :].unsqueeze(2).to_broadcast(wide), ALU.mult))
                link(dve.tensor_scalar(wn16[:, :, :], wn16[:, :, :], WMAX, -WMAX - 1.0, ALU.min, ALU.max))
                dve.tensor_tensor(wf_sb[:, :, :], wn16[:, :, :],
                                  wabs[:, 1, :].unsqueeze(2).to_broadcast(wide), ALU.mult).then_inc(wq_r, 1)

            def norm_stats(kind, layer, b):
                k = norm_no[kind, layer, b]
                if (kind, layer) == ("pre", 0):
                    dve.wait_ge(x_in[b], 16)
                elif kind == "pre":
                    dve.wait_ge(x2_r, b + 1)
                else:
                    dve.wait_ge(res_r, B * layer + b + 1)
                for t in range(TT):
                    ins = dve.bn_stats(stat6[:, k % 4, t, :], xr[:, TT * b + t, :])
                link(ins)
                for t in range(TT):
                    ins = dve.bn_aggr(mv[:, k % 4, t, :], stat6[:, k % 4, t, :])
                ins.then_inc(mv_r, 1)

            def norm(kind, layer, b):
                k = norm_no[kind, layer, b]
                dve.wait_ge(mv_r, k + 1)
                dve.wait_ge(rstd_r, k + 1)
                if B * layer + b > 0:
                    dve.wait_ge(xnT_r, norm_no[kind, (B * layer + b - 1) // B, (b - 1) % B] + 1)
                for t in range(TT):
                    ins = dve.tensor_scalar(xn[:, kind == "post", t, :], xr[:, TT * b + t, :], mv[:, k % 4, t, 0:1],
                                            rstd[:, k % 4, t:t + 1], ALU.subtract, ALU.mult)
                ins.then_inc(xn_r, 1)
                if (kind, layer) == ("post", 0):
                    dve.wait_ge(xn_r, k + 1)
                    dve.tensor_reduce(amax[:, 0, b:b + 1], xn[:, 1, :, :], AX.XY, ALU.max,
                                      apply_absolute_value=True).then_inc(am_r, 1)

            def q_low(layer, b):
                n = B * layer + b
                dve.wait_ge(qh_r, n + 1)
                if n >= 2:
                    dve.wait_ge(q_in[(n - 2) % 3], 12 * 16 * ((n - 2) // 3 + 1))
                dve.scalar_tensor_tensor(out=ql[:, n % 2, :], in0=misc[:, :],
                                         scalar=cols_sb[:, BQ + layer:BQ + layer + 1],
                                         in1=qh[:, n % 2, :].bitcast(F32), op0=ALU.add,
                                         op1=ALU.subtract).then_inc(ql_r, 1)

            def take_top(layer, b, u):
                k = units_before(B * layer + b) + u
                qt, h0, heads, keys = UNITS[layer][u]
                dve.wait_ge(top_r, k + 1)
                dve.tensor_reduce(nm[:, qt, h0:h0 + heads],
                                  top[k % MRING][:, 0:keys * heads].rearrange("p (h k) -> p h k", h=heads),
                                  AX.X, ALU.max, negate=True).then_inc(top_red, 1)

            def split_top(layer, b):
                n = B * layer + b
                dve.wait_ge(top_red, units_before(n + 1))
                src = nm[:, :, :].rearrange("p t (j g) -> p (t j) g", g=G)
                part = [nms[:, :, :, a, :].rearrange("p t j g -> p (t j) g") for a in range(2)]
                if n > 0:
                    dve.wait_ge(nmT_r, n)
                dve.tensor_copy(part[0], src).then_inc(nmh_r, 1)
                dve.wait_ge(nmh_r, n + 1)
                dve.tensor_tensor(part[1], src, part[0].bitcast(F32), ALU.subtract).then_inc(nms_r, 1)

            def divide(layer, b):
                n = B * layer + b
                for a in range(2):
                    dve.wait_ge(pv_r, ROUNDS * n + 5 + a)
                    dve.transpose(oq[:, a, :, :, :].rearrange("p k e r -> p (k e r)"), pv[a][:, :]).then_inc(pvx, 1)
                    dve.wait_ge(pvx, 2 * n + a + 1)
                link(dve.reciprocal(orc[:, :, :, :].rearrange("p a k e -> p (a k) e"),
                                    oq[:, :, :, :, D].rearrange("p a k e -> p (a k) e")))
                for a in range(2):
                    link(dve.tensor_tensor(oc[:, :, a, :, :], oq[:, a, :, :, 0:D],
                                           orc[:, a, :, :].unsqueeze(3).to_broadcast([P, T // 32, 2, D]), ALU.mult))
                if n > 0:
                    dve.wait_ge(misc_full, use["wo", (n - 1) // B, (n - 1) % B] + 1)
                dve.transpose(oT[:, :], oc[:, :, :, :, :].rearrange("p k a e d -> p (k a e d)")).then_inc(oT_r, 1)

            def residual(layer, b):
                n = B * layer + b
                dve.wait_ge(misc_full, use["wo", layer, b] + 1)
                dve.wait_ge(xg_r, n + 1)
                dve.scalar_tensor_tensor(out=xr[:, TT * b:TT * b + TT, :].rearrange("p t c -> p (t c)"),
                                         in0=misc[:, :], scalar=tg[:, layer:layer + 1],
                                         in1=xg[:, n % 2, :, :].rearrange("p t c -> p (t c)"),
                                         op0=ALU.mult, op1=ALU.add).then_inc(res_r, 1)

            def update(b):
                dve.wait_ge(gt_r, 3 * b + 1)
                dve.scalar_tensor_tensor(out=tmp[:, 0, :], in0=gt[:, 0, :], scalar=1.0, in1=cst[:, :],
                                         op0=ALU.add, op1=ALU.mult).then_inc(ct_r, 1)
                dve.wait_ge(gt_r, 3 * b + 3)
                dve.scalar_tensor_tensor(out=tmp[:, 1, :], in0=gt[:, 1, :], scalar=1.0, in1=gt[:, 2, :],
                                         op0=ALU.add, op1=ALU.mult).then_inc(ct_r, 1)
                dve.wait_ge(ct_r, 2 * b + 2)
                dve.scalar_tensor_tensor(out=cst[:, :], in0=tmp[:, 0, :], scalar=0.5, in1=tmp[:, 1, :],
                                         op0=ALU.mult, op1=ALU.add).then_inc(c_r, 1)

            def global_scale(k, n_parts, raw=1.0, raw_ap=()):
                dve.wait_ge(am_r, am_count[k])
                dve.tensor_reduce(amx[:, k:k + 1], amax[:, k, 0:n_parts], AX.X, ALU.max).then_inc(amx_r, 1)
                dve.wait_ge(misc_full, use["gt", k] + 1)
                dve.tensor_reduce(gtop[0:1, k:k + 1], misc[0:1, 0:P], AX.X, ALU.max).then_inc(gtop_r, 1)
                dve.wait_ge(gtop_r, k + 1)
                dve.wait_ge(misc_full, use["gb", k] + 1)
                dve.tensor_scalar(sc[:, k, 0:1], misc[:, 0:1], raw, None, ALU.mult).then_inc(smax_r, 1)
                dve.wait_ge(smax_r, k + 1)
                for ap in raw_ap:
                    link(dve.tensor_scalar(sc[:, k, 0:1], sc[:, k, 0:1], ap, None, ALU.mult))
                link(dve.tensor_scalar(sc[:, k, 1:2], sc[:, k, 0:1], 1.0 / QMAX, SMIN, ALU.mult, ALU.max))
                link(dve.reciprocal(sc[:, k, 2:3], sc[:, k, 1:2]))
                src = sc[:, k, 1:2] if k == 1 else sc[:, k, 2:3]
                for ap in raw_ap:
                    link(dve.tensor_scalar(sc[:, k, 3:4], src, ap, None, ALU.mult))
                    src = sc[:, k, 3:4]
                dve.tensor_scalar(sc[:, k, 3:4], src, 0.5 if k == 1 else raw, None, ALU.mult).then_inc(sc_r, 1)
                dve.wait_ge(sc_r, k + 1)

            def ffn():
                flat = lambda t, c: t[:, c, :, :].rearrange("p m t -> p (m t)")
                global_scale(0, B)
                for c in range(B):
                    dve.wait_ge(xnT_r, norm_no["post", 0, B - 1] + 1)
                    dve.tensor_scalar(n16[:, c, :], pnT[:, c, :], sc[:, 0, 2:3], None, ALU.mult).then_inc(n16_r, 1)
                    dve.wait_ge(n16_r, c + 1)
                    dve.tensor_scalar(xq[:, c, :], n16[:, c, :], sc[:, 0, 1:2], None, ALU.mult).then_inc(xq_r, 1)

                def absmax(k, t, src):
                    dve.wait_ge(fev, t + 1)
                    dve.tensor_reduce(amax[:, k, t % 12:t % 12 + 1], src[:, t % 12 // 3, t % 3, :], AX.X, ALU.max,
                                      apply_absolute_value=True).then_inc(am_r, 1)

                for t in range(12):
                    absmax(1, t, gf)
                global_scale(1, 12)
                for c in range(B):
                    dve.tensor_scalar(flat(g16, c), flat(gf, c), sc[:, 1, 2:3], None, ALU.mult).then_inc(g16_r, 1)
                    for t in range(12 + 3 * c, 15 + 3 * c):
                        absmax(2, t, uf)
                global_scale(2, 12)
                for c in range(B):
                    dve.wait_ge(th_r, c + 1)
                    dve.tensor_scalar(flat(s16, c), flat(gf, c), 32768.0, 32768.0, ALU.mult, ALU.add).then_inc(s16_r, 1)
                    dve.wait_ge(s16_r, c + 1)
                    dve.tensor_tensor(flat(gf, c), flat(g16, c), flat(s16, c), ALU.mult).then_inc(g2_r, 1)
                    dve.wait_ge(g2_r, c + 1)
                    dve.tensor_reduce(amax[:, 3, c:c + 1], flat(gf, c), AX.X, ALU.max,
                                      apply_absolute_value=True).then_inc(am_r, 1)
                global_scale(3, B, 2.0 ** -16, (sc[:, 1, 1:2],))
                for c in range(B):
                    dve.tensor_scalar(flat(g16, c), flat(gf, c), sc[:, 3, 3:4], None, ALU.mult).then_inc(n2_r, 1)
                    dve.wait_ge(n2_r, c + 1)
                    dve.wait_ge(u16_r, c + 1)
                    dve.tensor_tensor(flat(uf, c), flat(g16, c), flat(u16, c), ALU.mult).then_inc(o_r, 1)
                    dve.wait_ge(o_r, c + 1)
                    dve.tensor_reduce(amax[:, 4, c:c + 1], flat(uf, c), AX.X, ALU.max,
                                      apply_absolute_value=True).then_inc(am_r, 1)
                global_scale(4, B, 1.0, (sc[:, 3, 1:2], sc[:, 2, 1:2]))
                for c in range(B):
                    dve.tensor_scalar(flat(g16, c), flat(uf, c), sc[:, 4, 3:4], None, ALU.mult).then_inc(n3_r, 1)
                for c in range(B):
                    dve.wait_ge(dmm, c + 1)
                    xc = xr[:, TT * c:TT * c + TT, :].rearrange("p t c -> p (t c)")
                    dve.scalar_tensor_tensor(out=xc, in0=fbank[c][:, :], scalar=tg[:, 2:3], in1=xc,
                                             op0=ALU.mult, op1=ALU.add).then_inc(x2_r, 1)

            am_count = {0: 4, 1: 16, 2: 28, 3: 32, 4: 36}

            dve.memset(ones[:, :], 1.0).then_inc(ones_r, 1)
            dve.wait_ge(ones_r, 1)
            dve.wait_ge(small_in, 48)
            dve.wait_ge(gates, 1)
            for n in range(2):
                dve.tensor_scalar(bog[:, n, :], rows_sb[:, RO + n, :], tg[:, n:n + 1], None, ALU.mult).then_inc(bias_r, 1)
            for n in range(2):
                link(dve.tensor_scalar(bvt[:, n, :], rows_sb[:, RV + n, :], own[:, 0:1], None, ALU.mult))
            norm_stats("pre", 0, 0)
            keys(0)
            values(0)

            for layer in range(2):
                for i in range(-2, B + 1):
                    for slot in range(SLOTS):
                        if slot == 0 and 0 <= i - 1 < B:
                            divide(layer, i - 1)
                        if 0 <= i + 1 < B:
                            for u in units_at(layer, slot):
                                take_top(layer, i + 1, u)
                        if slot == 5 and 0 <= i + 2 < B and (layer, i) != (0, -2):
                            norm_stats("pre", layer, i + 2)
                        for name, b in events(i, slot):
                            if name == "wo":
                                residual(layer, b)
                                norm_stats("post", layer, b)
                            if name in ("pre", "post"):
                                norm(name, layer, b)
                            if name == "q":
                                q_low(layer, b)
                            if name == "post" and layer == 1:
                                update(b)
                            if name == "top":
                                split_top(layer, b)
                    if layer == 0 and i == -2:
                        tail_keys(0)
                        weights()
                    if layer == 0 and i == -1:
                        keys(1)
                        values(1)
                        tail_keys(1)
                        dve.tensor_scalar(cst[:, :].rearrange("p (t c) -> p t c", c=P),
                                          ones[:, :].unsqueeze(1).to_broadcast([P, TT, P]),
                                          cols_sb[:, INC:INC + 1], 2.0, ALU.mult, ALU.mult).then_inc(c_r, 1)
                        dve.wait_ge(wl_in, 16)
                        for wu in (UF, UI, UC, UOUT):
                            ins = dve.tensor_scalar(wsb[:, wu, :], wsb[:, wu, :], 0.5, None, ALU.mult)
                        ins.then_inc(c_r, 1)
                if layer == 0:
                    ffn()
            for b in range(B):
                dve.wait_ge(y_r, b + 1)
                yb = yt[:, b, :, :].rearrange("p t c -> p (t c)")
                dve.scalar_tensor_tensor(out=yb, in0=yb, scalar=tg[:, 3:4],
                                         in1=xr[:, TT * b:TT * b + TT, :].rearrange("p t c -> p (t c)"),
                                         op0=ALU.mult, op1=ALU.add).then_inc(out_r, 1)


_WEIGHTS = ["L0_xattn_Wq", "L0_xattn_Wk", "L0_xattn_Wv", "L0_xattn_Wo", "L1_xattn_Wq", "L1_xattn_Wk", "L1_xattn_Wv",
            "L1_xattn_Wo", "L1_ffn_wf", "L1_ffn_uf", "L1_ffn_wi", "L1_ffn_ui", "L1_ffn_wc", "L1_ffn_uc", "L1_ffn_wo",
            "L1_ffn_uo"]


def constants():
    a = np.arange(P)
    ident = np.eye(P)
    top = np.where(a[None, :] > a[:, None], NEG, 0.0)
    main = np.where(a[:, None] > a[None, :], NEG, 0.0)
    tail = np.where((a % 32)[:, None] > np.arange(32)[None, :] + OWN, NEG, 0.0)
    own = (a % 32 >= OWN)[:, None]
    return np.concatenate([ident, top, main, tail, own], axis=1).astype(np.float32)


def kernel(**inputs):
    import concourse.bacc as bacc
    from concourse.bass_utils import run_bass_kernel_spmd

    order = np.arange(C).reshape(G, J, D).transpose(1, 2, 0).reshape(-1)
    turned = []
    for name in _WEIGHTS:
        t = np.asarray(inputs[name]).T
        turned.append(t[:, order] if name.endswith(("Wq", "Wk")) else t)
    ctx = np.asarray(inputs["ctx_1024"]).transpose(2, 0, 1)
    tail = np.zeros((C, B, 4, 32), np.float32)
    tail[:, :, :, OWN:] = ctx[:, :, None, P:]
    wffn = [np.asarray(inputs[f"L0_ffn_w_{n}"]).reshape(NF, P, C).transpose(1, 0, 2).reshape(P, -1) for n in ("gate", "up")]
    wffn.append(np.asarray(inputs["L0_ffn_w_down"]))
    cols = [np.asarray(inputs[f"{n}"])[order] for n in ("L0_xattn_bq", "L1_xattn_bq", "L0_xattn_bk", "L1_xattn_bk")]
    cols += [np.asarray(inputs[f"L1_ffn_{n}"]) for n in ("bf", "bi", "bc", "in_c")]
    gates = np.zeros(C, np.float32)
    gates[0:2], gates[2:4] = inputs["g_xattn"], inputs["g_ffn"]
    rows = [np.asarray(inputs[n]) for n in ("L0_xattn_bv", "L1_xattn_bv", "L0_xattn_bo", "L1_xattn_bo", "L1_ffn_bo")]
    arrays = {
        "x": np.asarray(inputs["x"]),
        "w": np.stack(turned, axis=1),
        "ctxT": ctx,
        "tailT": tail.reshape(C, B, P),
        "wffn": np.concatenate(wffn, axis=1).reshape(P, NBLK, 32),
        "cols": np.stack(cols, axis=1),
        "rows": np.stack(rows + [gates], axis=0),
        "consts": constants(),
    }
    arrays = {k: np.ascontiguousarray(v) for k, v in arrays.items()}
    nc = bacc.Bacc("TRN2", target_bir_lowering=False, num_devices=1)
    args = [nc.dram_tensor(k, v.shape, F32, kind="ExternalInput").ap() for k, v in arrays.items()]
    out = nc.dram_tensor("out", (B, T, C), F32, kind="ExternalOutput").ap()
    program(nc, *args, out)
    result = run_bass_kernel_spmd(nc, [arrays], core_ids=[0])
    return result.results[0]["out"]
```

```python
from contextlib import ExitStack

import numpy as np

import concourse.bass as bass
from concourse import mybir

F32 = mybir.dt.float32
F32R = mybir.dt.float32r
I16 = mybir.dt.int16
U16 = mybir.dt.uint16
ALU = mybir.AluOpType
ACT = mybir.ActivationFunctionType
AX = mybir.AxisListType

P = 128
B, T, C = 4, 512, 128
TT = T // P
S = 154
H, D = 16, 8
G, J = 4, 4
NF = 3
TAIL0 = S - 32
OWN = P - TAIL0
SCALE = float(D) ** -0.5
EPS = 1e-5
NEG = -2.0 ** 126
QMAX = 32767.0
WMAX = 7.0
SMIN = 1e-12
NBLK = 36

PARTS = 4

SLOTS = 20
TILES = H + G
ROUNDS = 6
EARLY, LAST = 3, 13
PRING = 8
SRING = 2
MRING = 3
FRING = 7

WQ, WV, WO = 0, 1, 2
WL1 = 3
WF, UF, WI, UI, WC, UC, WOUT, UOUT = range(6, 14)
NW = 14
BQ, BF, BI, BC, INC, BK = 0, 2, 3, 4, 5, 6
NCOL = BK + 2 * G
RV, RO, RFO, RG = 0, 2, 4, 5


def max_units(layer):
    units = []
    for qt in range(TT):
        heads, keys = (J, P) if layer == 1 and qt == 0 else (J // 2, S)
        units += [(qt, h, heads, keys) for h in range(0, H, heads)]
    return units


UNITS = [max_units(0), max_units(1)]


def units_at(layer, i, slot):
    n = len(UNITS[layer])
    share = lambda k: range(n * k // (EARLY + LAST), n * (k + 1) // (EARLY + LAST))
    taken = []
    if slot < LAST and 0 <= i + 1 < B:
        first = 0 if (i, slot) == (-1, 0) else slot + EARLY
        taken += [(i + 1, u) for k in range(first, slot + EARLY + 1) for u in share(k)]
    if slot >= SLOTS - EARLY and i + 2 < B:
        taken += [(i + 2, u) for u in share(slot - SLOTS + EARLY)]
    return taken


def units_before(n):
    return sum(len(UNITS[m // B]) for m in range(n))


PE_PLAN = [(1, "tail0", -1), (2, "tail1", -1), (6, "round0", 0), (7, "wo", -1), (9, "pre", 2), (9, "round1", 0),
           (11, "q", 2), (13, "round2", 0), (14, "top", 1), (15, "post", -1), (17, "step0", -1), (17, "round3", 0),
           (18, "step1", -1), (19, "step2", -1)]
ACT_PLAN = [(10, "pre", 2), (12, "q", 2), (14, "top", 1), (16, "post", -1), (17, "step0", -1), (18, "step1", -1),
            (19, "step2", -1)]
DVE_PLAN = [(1, "stat pre", 2), (3, "div0", -1), (4, "div1", -1), (5, "div2", -1), (6, "div3", -1), (7, "pre", 2),
            (8, "wo", -1), (9, "stat post", -1), (12, "q", 2), (13, "top", 1), (14, "post", -1), (16, "amax", -1),
            (19, "step", -1)]
MISC_USERS = ("wo", "pre", "q", "post", "top", "step0", "step1", "step2")


def planned(plan, layer, i, slot):
    for at, what, shift in plan:
        if at == slot and 0 <= i + shift < B and (layer == 1 or not what.startswith("step")) and (layer == 0 or what != "amax"):
            yield what, i + shift


def norm_order():
    order = []
    for layer in range(2):
        for i in range(-2, B + 1):
            order += [(kind, layer, b) for kind, b in (("pre", i + 2), ("post", i - 1)) if 0 <= b < B]
    return order


NORMS = norm_order()
norm_no = {name: k for k, name in enumerate(NORMS)}


def misc_plan():
    order = []
    for layer in range(2):
        for i in range(-2, B + 1):
            for slot in range(SLOTS):
                order += [(what, layer, b) for what, b in planned(PE_PLAN, layer, i, slot) if what in MISC_USERS]
            if layer == 0 and i == -1:
                order += [("w", 0), ("w", 1), ("w", 2)]
        if layer == 0:
            for k in range(5):
                order += [("gt", k), ("gb", k)]
    return order


def program(nc, x, w, wkr, ctxT, tailT, wffn, cols, rows, consts, out):
    with ExitStack() as ctx:
        def sb(name, shape, dt=F32):
            return ctx.enter_context(nc.sbuf_tensor("sb_" + name, shape, dt))

        def bank(name):
            return ctx.enter_context(nc.psum_tensor("ps_" + name, [P, 512], F32))

        def sem(name):
            return ctx.enter_context(nc.semaphore(name))

        xr = sb("xr", [P, B * TT, C])
        wsb = sb("wsb", [P, NW, C])
        ctx_sb = sb("ctx", [P, B, S])
        tail_sb = sb("tail", [P, B, P])
        wf_sb = sb("wf", [P, NBLK, 32])
        wabs = sb("wabs", [P, 3, NBLK])
        wkr_sb = sb("wkr", [P, 2, G, P])
        wfT = sb("wfT", [P, 9, C])
        cols_sb = sb("cols", [P, NCOL])
        lcols = sb("lcols", [P, 2 * G])
        hcols = sb("hcols", [P, NCOL])
        rows_sb = sb("rows", [P, 6, C])
        tg = sb("tg", [P, 4])
        bog = sb("bog", [P, 2, C])
        bvt = sb("bvt", [P, 2, C])
        consts_sb = sb("consts", [P, 3 * P + 35])
        ident = consts_sb[:, 0:P]
        cmask = consts_sb[:, P:3 * P + 32]
        own = consts_sb[:, 3 * P + 32:3 * P + 33]
        lowrow = consts_sb[:, 3 * P + 33:3 * P + 34]
        keyrow = consts_sb[:, 3 * P + 34:3 * P + 35]
        identr = sb("identr", [P, P], F32R)
        maskr = sb("maskr", [P, 2 * P + 32], F32R)
        maskM, maskT, maskE = maskr[:, 0:P], maskr[:, P:2 * P], maskr[:, 2 * P:2 * P + 32]
        ones = sb("ones", [P, P])
        stat6 = sb("stat6", [P, 4, TT, 6])
        mv = sb("mv", [P, 4, TT, 2])
        var = sb("var", [P, 4, TT])
        half = sb("half", [P, TT])
        rstd = sb("rstd", [P, 4, TT])
        xn = sb("xn", [P, 2, TT, C])
        pnT = sb("pnT", [P, B, T])
        K4 = sb("K4", [P, G, B, S], F32R)
        KT = sb("KT", [P, B, G, P], F32R)
        V4 = sb("V4", [P, B, G, J, 32])
        VT = sb("VT", [P, B, G, 64])
        kf = sb("kf", [P, 2, 308])
        kh = sb("kh", [P, 2, 308], F32R)
        tmp = sb("tmp", [P, 2, T])
        vf = tmp
        nm = sb("nm", [P, TT, H])
        nms = sb("nms", [P, TT, 2, J, G], F32R)
        orc = sb("orc", [P, 2, T // 32, 2])
        amax = sb("amax", [P, 5, 12])
        amx = sb("amx", [P, 5])
        gtop = sb("gtop", [1, 5])
        sc = sb("sc", [P, 5, 4])
        cst = sb("cst", [P, T])

        with ExitStack() as stretch:
            def sb_here(name, shape, dt=F32):
                return stretch.enter_context(nc.sbuf_tensor("sb_" + name, shape, dt))

            Q4 = [sb_here(f"Q4{n}", [P, G, T], F32R) for n in range(3)]
            Kd = [sb_here(f"Kd{n}", [P, G, J, S], F32R) for n in range(2)]
            qh = sb_here("qh", [P, 2, T], F32R)
            pr = sb_here("pr", [P, PRING, T])
            oq = sb_here("oq", [P, 2, T // 32, 2, 16])
            oc = sb_here("oc", [P, T // 32, 2, 2, D])
            oT = sb_here("oT", [P, T])
            gt = sb_here("gt", [P, 3, T])
            wn16 = gt[:, :, :].rearrange("p k t -> p (k t)").bitcast(I16)[:, 0:NBLK * 32].rearrange("p (n c) -> p n c", c=32)
            yt = pr[:, 0:B, :].rearrange("p b (t c) -> p b t c", c=C)
            ql = sb_here("ql", [P, 2, T], F32R)
            nmT = sb_here("nmT", [32, 2, T], F32R)
            xnT = sb_here("xnT", [P, T])
            xg = sb_here("xg", [P, 2, TT, C])
        with ExitStack() as stretch:
            def sb_here(name, shape, dt=F32):
                return stretch.enter_context(nc.sbuf_tensor("sb_" + name, shape, dt))

            s16 = sb_here("s16", [P, B, NF, T], U16)
            u16 = sb_here("u16", [P, B, NF, T], I16)
            uf = sb_here("uf", [P, B, NF, T])
            gf = sb_here("gf", [P, B, NF, T])
            g16 = sb_here("g16", [P, B, NF, T], I16)
            n16 = sb_here("n16", [P, B, T], I16)
            xq = sb_here("xq", [P, B, T])

        score = [bank(f"score{n}") for n in range(SRING)]
        top = [bank(f"top{n}") for n in range(MRING)]
        pv = [bank(f"pv{n}") for n in range(2)]
        misc = bank("misc")
        fbank = score + top + pv
        kbank = score + top

        x_in = [sem(f"x_in{b}") for b in range(B)]
        w_in, small_in, k_in, tail_in, wl_in, wf_in = (
            sem(n) for n in ("w_in", "small_in", "k_in", "tail_in", "wl_in", "wf_in"))
        const_r = sem("const_r")
        gates = sem("gates")
        hcol_r, lcol_r = sem("hcol_r"), sem("lcol_r")
        bias_r = sem("bias_r")
        ones_r, half_r = sem("ones_r"), sem("half_r")
        q4_clear, kd_clear = sem("q4_clear"), sem("kd_clear")
        zero_r = sem("zero_r")
        misc_full = sem("misc_full")
        kmm, vmm = sem("kmm"), sem("vmm")
        kf_r, kh_r, k4_r = sem("kf_r"), sem("kh_r"), sem("k4_r")
        kd_r = sem("kd_r")
        kt_r = sem("kt_r")
        v_r, vf_r = sem("v_r"), sem("vf_r")
        stats_r, mv_r, var_r, rstd_r, xn_r, xnT_r = (sem(n) for n in ("stats_r", "mv_r", "var_r", "rstd_r", "xn_r", "xnT_r"))
        qh_r, ql_r = sem("qh_r"), sem("ql_r")
        q_in = [sem(f"q_in{n}") for n in range(3)]
        m_in = [sem(f"m_in{n}") for n in range(3)]
        top_r, top_red = sem("top_r"), sem("top_red")
        nmh_r, nms_r, nmT_r = sem("nmh_r"), sem("nms_r"), sem("nmT_r")
        score_r, exp_r, pv_r = sem("score_r"), sem("exp_r"), sem("pv_r")
        pvx = sem("pvx")
        orc_r, oc_r, oT_r = sem("orc_r"), sem("oc_r"), sem("oT_r")
        xg_r, res_r = sem("xg_r"), sem("res_r")
        wq_r, wT_r = sem("wq_r"), sem("wT_r")
        fmm, fev = sem("fmm"), sem("fev")
        am_r, amx_r, gtop_r, sc_r = sem("am_r"), sem("amx_r"), sem("gtop_r"), sem("sc_r")
        xq_r, g16_r, th_r, s16_r, g2_r, n2_r, u16_r, o_r, n3_r, xo_r = (
            sem(n) for n in ("xq_r", "g16_r", "th_r", "s16_r", "g2_r", "n2_r", "u16_r", "o_r", "n3_r", "xo_r"))
        n16_r, smax_r = sem("n16_r"), sem("smax_r")
        s16a_r, n2a_r = sem("s16a_r"), sem("n2a_r")
        xod_r = sem("xod_r")
        dmm, x2_r = sem("dmm"), sem("x2_r")
        gt_r, ct_r, c_r = sem("gt_r"), sem("ct_r"), sem("c_r")
        ymm, y_r, out_r, out_in = sem("ymm"), sem("y_r"), sem("out_r"), sem("out_in")

        misc_uses = misc_plan()
        use = {name: n for n, name in enumerate(misc_uses)}

        def misc_read(name):
            kind = name[0]
            if kind in ("pre", "post"):
                return xnT_r, norm_no[name] + 1
            if kind == "q":
                return ql_r, B * name[1] + name[2] + 1
            if kind == "top":
                return nmT_r, B * name[1] + name[2] + 1
            if kind == "wo":
                return res_r, B * name[1] + name[2] + 1
            if kind.startswith("step"):
                return gt_r, 3 * name[2] + int(kind[4]) + 1
            if kind == "w":
                return wT_r, name[1] + 1
            return (gtop_r if kind == "gt" else smax_r), name[1] + 1

        block = ctx.enter_context(nc.Block())

        def fill_misc(pe, name):
            if use[name] > 0:
                pe.wait_ge(*misc_read(misc_uses[use[name] - 1]))

        def weight(n):
            return wsb[:, n, :]

        @block.sync
        def _(sp):
            xd = x.rearrange("b (t p) c -> p b t c", p=P)
            sp.dma_start(xr[:, 0:TT, :], xd[:, 0]).then_inc(x_in[0], 16)
            sp.dma_start(ctx_sb[:, :, :], ctxT).then_inc(k_in, 16)
            sp.dma_start(wkr_sb[:, :, :, :], wkr).then_inc(k_in, 16)
            sp.dma_start(wsb[:, 0:WL1, :], w[:, 0:WL1, :]).then_inc(w_in, 16)
            sp.dma_start(tail_sb[:, :, :], tailT).then_inc(tail_in, 16)
            for b in range(1, B):
                sp.dma_start(xr[:, TT * b:TT * b + TT, :], xd[:, b]).then_inc(x_in[b], 16)
            sp.dma_start(wf_sb[:, :, :], wffn).then_inc(wf_in, 16)
            sp.dma_start(wsb[:, WL1:NW, :], w[:, WL1:NW, :]).then_inc(wl_in, 16)

            def queries(layer, b):
                n = B * layer + b
                sp.wait_ge(q4_clear, 3 * layer + min(b, 2) + 1)
                if n >= 3:
                    sp.wait_ge(score_r, TILES * (n - 2))
                for a, (src, ready) in enumerate(((qh, qh_r), (ql, ql_r), (qh, qh_r))):
                    sp.wait_ge(ready, n + 1)
                    sp.dma_start(Q4[n % 3][a:P:PARTS, :, :].bitcast(F32),
                                 src[:, n % 2, :].bitcast(F32)).then_inc(q_in[n % 3], 16)

            def tops(layer, b):
                n = B * layer + b
                sp.wait_ge(nmT_r, n + 1)
                for a in range(2):
                    sp.dma_start(Q4[n % 3][3 + PARTS * a:P:32, :, :].bitcast(F32),
                                 nmT[16 * a:16 * a + 16, n % 2, :].bitcast(F32)).then_inc(m_in[n % 3], 16)

            for layer in range(2):
                for i in range(-2, B + 1):
                    if 0 <= i + 2 < B:
                        queries(layer, i + 2)
                    if 0 <= i + 1 < B:
                        tops(layer, i + 1)
            od = out.rearrange("b (t p) c -> p b t c", p=P)
            for b in range(B):
                sp.wait_ge(out_r, b + 1)
                sp.dma_start(od[:, b], xr[:, TT * b:TT * b + TT, :]).then_inc(out_in, 16)
            sp.wait_ge(out_in, 16 * B)

        @block.gpsimd
        def _(pool):
            chained = [0]
            chain = ctx.enter_context(nc.semaphore("pool_chain"))

            def link(ins):
                chained[0] += 1
                ins.then_inc(chain, 1)
                pool.wait_ge(chain, chained[0])

            pool.memset(half[:, :], -0.5).then_inc(half_r, 1)


            def clear(layer):
                if layer == 1:
                    pool.wait_ge(o_r, B)
                    for b in range(3):
                        pool.memset(Q4[(B + b) % 3][:, :, :].bitcast(F32), 0.0).then_inc(q4_clear, 1)
                    pool.wait_ge(n3_r, B)
                for n in range(2):
                    pool.memset(Kd[n][:, :, :, :].bitcast(F32), 0.0).then_inc(kd_clear, 1)

            def keys_late():
                for g in range(G):
                    for part in range(2):
                        k = 2 * (G + g) + part
                        pool.wait_ge(kf_r, k + 1)
                        pool.wait_ge(kh_r, k + 1)
                        if k == 2 * G:
                            pool.wait_ge(score_r, TILES * B)
                        dst = K4[:, g, 2 * part:2 * part + 2, :].rearrange("p b s -> p (b s)")
                        pool.tensor_tensor(dst, kf[:, k % 2, :], kh[:, k % 2, :].bitcast(F32), ALU.subtract)\
                            .then_inc(k4_r, 1)

            def diagonal(layer, b):
                n = B * layer + b
                pool.wait_ge(top_r, units_before(n - 1))
                for j in range(J):
                    q = slice(32 * j, 32 * j + 32)
                    ins = pool.tensor_scalar(Kd[n % 2][q, :, j, :], K4[q, :, b, :].bitcast(F32), keyrow[q, 0:1], 1.0,
                                             ALU.mult, ALU.mult)
                    if j < J - 1:
                        link(ins)
                ins.then_inc(kd_r, 1)
                pool.wait_ge(kd_r, n + 1)

            def tail_keys(layer):
                pool.wait_ge(k4_r, 8 * layer + 8)
                for j in range(J):
                    q = slice(32 * j, 32 * j + 32)
                    ins = pool.tensor_copy(KT[q, :, :, 32 * j:32 * j + 32],
                                           K4[q, :, :, TAIL0:S].rearrange("p g b s -> p b g s"))
                    if j < J - 1:
                        link(ins)
                ins.then_inc(kt_r, 1)
                pool.wait_ge(kt_r, layer + 1)

            def frames():
                pool.memset(V4[:, :, :, :, :], 0.0).then_inc(zero_r, 1)
                pool.memset(VT[:, :, :, :], 0.0).then_inc(zero_r, 1)
                pool.memset(KT[:, :, :, :].bitcast(F32), 0.0).then_inc(zero_r, 1)
                pool.wait_ge(zero_r, 3)
                pool.wait_ge(ones_r, 1)
                pool.wait_ge(small_in, 48)
                for j in range(J):
                    c = 16 * (j % 2) + D
                    for b in range(B):
                        ins = pool.memset(V4[:, b, :, j, c:c + D], 1.0)
                    link(ins)
                    q = slice(32 * j, 32 * j + 32)
                    on = ones[q, :].rearrange("p (b g d) -> p b g d", b=B, g=G)
                    link(pool.tensor_scalar(VT[q, :, :, 16 * j + D:16 * j + 2 * D], on, own[q, 0:1], 1.0,
                                            ALU.mult, ALU.mult))

            def values(layer):
                V, E = V4, VT
                if layer == 1:
                    pool.wait_ge(pv_r, ROUNDS * B)
                pool.wait_ge(bias_r, 4)
                for t, bias, dst in ((0, rows_sb[:, RV + layer, :], V), (1, bvt[:, layer, :], E)):
                    pool.wait_ge(vf_r, 2 * layer + t + 1)
                    src = vf[:, t, :].rearrange("p (b g j d) -> p b g j d", b=B, g=G, j=J)
                    bias = bias.rearrange("p (g j d) -> p g j d", g=G, j=J)
                    for j in range(J):
                        for b in range(B):
                            if t == 0:
                                ins = pool.tensor_tensor(V[:, b, :, j, 16 * (j % 2):16 * (j % 2) + D], src[:, b, :, j, :],
                                                         bias[:, :, j, :], ALU.add)
                            else:
                                q = slice(32 * j, 32 * j + 32)
                                ins = pool.tensor_tensor(E[q, b, :, 16 * j:16 * j + D], src[q, b, :, j, :],
                                                         bias[q, :, j, :], ALU.add)
                                if (b, j) != (B - 1, J - 1):
                                    link(ins)
                    if t == 0:
                        link(ins)
                ins.then_inc(v_r, 1)
                pool.wait_ge(v_r, layer + 1)

            def biased(layer, b):
                n = B * layer + b
                if n >= 2:
                    pool.wait_ge(res_r, n - 1)
                if layer == 1:
                    pool.wait_ge(x2_r, b + 1)
                else:
                    pool.wait_ge(x_in[b], 16)
                pool.wait_ge(bias_r, 4)
                for t in range(TT):
                    ins = pool.tensor_tensor(xg[:, n % 2, t, :], xr[:, TT * b + t, :], bog[:, layer, :], ALU.add)
                ins.then_inc(xg_r, 1)

            def root(k):
                pool.wait_ge(mv_r, k + 1)
                pool.tensor_scalar(var[:, k % 4, :], mv[:, k % 4, :, 1], EPS, 1.0, ALU.add, ALU.mult).then_inc(var_r, 1)
                pool.wait_ge(var_r, k + 1)
                pool.tensor_tensor(rstd[:, k % 4, :], var[:, k % 4, :], half[:, :], ALU.pow).then_inc(rstd_r, 1)

            pool.wait_ge(half_r, 1)
            clear(0)
            for layer in range(2):
                root(norm_no["pre", layer, 0])
                root(norm_no["pre", layer, 1])
                if layer == 0:
                    for n in (1, 2):
                        pool.memset(Q4[n][:, :, :].bitcast(F32), 0.0).then_inc(q4_clear, 1)
                    frames()
                    values(0)
                    tail_keys(0)
                for i in range(-1, B + 1):
                    if 0 <= i + 2 < B and i >= 0:
                        root(norm_no["pre", layer, i + 2])
                        diagonal(layer, i + 2)
                    if 0 <= i - 1 < B:
                        root(norm_no["post", layer, i - 1])
                    if 0 <= i + 1 < B:
                        biased(layer, i + 1)
                if layer == 0:
                    keys_late()
                    values(1)
                    tail_keys(1)
                    clear(1)

        @block.scalar
        def _(act):
            act.dma_start(cols_sb[:, :], cols).then_inc(small_in, 16)
            act.dma_start(rows_sb[:, :, :], rows.partition_broadcast(P)).then_inc(small_in, 16)
            act.dma_start(consts_sb[:, :], consts).then_inc(small_in, 16)
            act.wait_ge(small_in, 48)
            act.activation(tg[:, :], rows_sb[:, RG, 0:4], ACT.Tanh).then_inc(gates, 1)
            act.activation(hcols[:, :], cols_sb[:, :], ACT.Copy, scale=0.5).then_inc(hcol_r, 1)
            act.activation(identr[:, :], ident[:, :], ACT.Copy).then_inc(const_r, 1)
            act.activation(maskr[:, :], cmask[:, :], ACT.Copy).then_inc(const_r, 1)

            def copy_k(layer):
                for g in range(G):
                    for part in range(2):
                        k = 2 * (G * layer + g) + part
                        act.wait_ge(kmm, k + 1)
                        if k >= 2:
                            act.wait_ge(k4_r, k - 1)
                        col = G * layer + g
                        act.activation(kf[:, k % 2, :], kbank[k % len(kbank)][:, 0:308], ACT.Identity,
                                       bias=cols_sb[:, BK + col:BK + col + 1]).then_inc(kf_r, 1)
                        act.activation(kh[:, k % 2, :], kbank[k % len(kbank)][:, 0:308], ACT.Identity, bias=lcols[:, col:col + 1],
                                       scale=lowrow).then_inc(kh_r, 1)

            def copy_v(layer):
                for t in range(2):
                    act.wait_ge(vmm, 2 * layer + t + 1)
                    act.activation(vf[:, t, :], pv[t][:, :], ACT.Copy).then_inc(vf_r, 1)

            def diagonal(layer, b):
                n = B * layer + b
                act.wait_ge(k4_r, 8 * layer + 8)
                act.wait_ge(kd_clear, 2 * layer + n % 2 + 1)
                for j in range(J):
                    q = slice(32 * j, 32 * j + 32)
                    ins = act.activation(Kd[n % 2][q, :, j, :], K4[q, :, b, :].bitcast(F32), ACT.Copy, scale=keyrow[q, 0:1])
                ins.then_inc(kd_r, 1)

            def copy_normed(kind, layer, b):
                act.wait_ge(misc_full, use[kind, layer, b] + 1)
                if kind == "pre":
                    if (layer, b) != (0, 0):
                        act.wait_ge(qh_r, B * layer + b)
                    dst = xnT[:, :]
                else:
                    dst = pnT[:, b, :]
                    if layer == 1:
                        act.wait_ge(n16_r, B)
                act.activation(dst, misc[:, :], ACT.Copy).then_inc(xnT_r, 1)

            def copy_q(layer, b):
                n = B * layer + b
                act.wait_ge(misc_full, use["q", layer, b] + 1)
                if n >= 2:
                    act.wait_ge(q_in[(n - 2) % 3], 3 * 16 * ((n - 2) // 3 + 1))
                act.activation(qh[:, n % 2, :], misc[:, :], ACT.Identity,
                               bias=cols_sb[:, BQ + layer:BQ + layer + 1]).then_inc(qh_r, 1)

            def copy_top(layer, b):
                n = B * layer + b
                act.wait_ge(misc_full, use["top", layer, b] + 1)
                if n >= 2:
                    act.wait_ge(m_in[(n - 2) % 3], 2 * 16 * ((n - 2) // 3 + 1))
                act.activation(nmT[:, n % 2, :], misc[0:32, :], ACT.Copy).then_inc(nmT_r, 1)

            def exps(layer, b, t):
                k = TILES * (B * layer + b) + t
                act.wait_ge(score_r, k + 1)
                if k >= PRING:
                    m, old = divmod(k - PRING, TILES)
                    act.wait_ge(pv_r, ROUNDS * m + (old // 4 + 1 if old < H else ROUNDS))
                q0 = P if layer == 1 and t >= H else 0
                act.activation(pr[:, k % PRING, q0:T], score[k % SRING][:, q0:T], ACT.Exp, scale=SCALE).then_inc(exp_r, 1)

            def gate_of(b, k):
                act.wait_ge(misc_full, use[f"step{k}", 1, b] + 1)
                if b > 0:
                    act.wait_ge(c_r, b + 2)
                bias = (hcols[:, BF:BF + 1], hcols[:, BI:BI + 1], cols_sb[:, BC:BC + 1])[k]
                act.activation(gt[:, k, :], misc[:, :], ACT.Tanh, bias=bias, scale=(0.5, 0.5, 1.0)[k]).then_inc(gt_r, 1)

            act.wait_ge(lcol_r, 1)
            copy_k(0)
            for layer in range(2):
                copy_normed("pre", layer, 0)
                copy_q(layer, 0)
                diagonal(layer, 0)
                if layer == 0:
                    copy_v(0)
                diagonal(layer, 1)
                for i in range(-1, B + 1):
                    for slot in range(SLOTS):
                        if 0 <= i < B and slot < TILES:
                            exps(layer, i, slot)
                        for what, b in planned(ACT_PLAN, layer, i, slot):
                            if what in ("pre", "post"):
                                copy_normed(what, layer, b)
                            elif what == "q":
                                copy_q(layer, b)
                            elif what == "top":
                                copy_top(layer, b)
                            else:
                                gate_of(b, int(what[4]))
                    if layer == 0 and i == -1:
                        for k in range(3):
                            n = min(4, 9 - 4 * k)
                            act.wait_ge(misc_full, use["w", k] + 1)
                            act.activation(wfT[:, 4 * k:4 * k + n, :], misc[:, 0:n * P], ACT.Copy).then_inc(wT_r, 1)
                if layer == 0:
                    for t in range(24):
                        act.wait_ge(fmm, t + 1)
                        dst = gf if t < 12 else uf
                        act.activation(dst[:, t % 12 // 3, t % 3, :], fbank[t % FRING][:, :], ACT.Copy).then_inc(fev, 1)
                        if t >= 20:
                            c = t - 20
                            act.wait_ge(g16_r, c + 1)
                            act.wait_ge(sc_r, 2)
                            act.activation(gf[:, c, :, :], g16[:, c, :, :], ACT.Tanh, scale=sc[:, 1, 3:4]).then_inc(th_r, 1)
                    for c in (1, 3):
                        act.wait_ge(th_r, c + 1)
                        act.activation(s16[:, c, :, :], gf[:, c, :, :], ACT.Copy, bias=32768.0, scale=32768.0)\
                           .then_inc(s16a_r, 1)
                    copy_k(1)
                    copy_v(1)
                    for c in range(B):
                        act.wait_ge(sc_r, 3)
                        act.activation(u16[:, c, :, :], uf[:, c, :, :], ACT.Copy, scale=sc[:, 2, 2:3]).then_inc(u16_r, 1)
                    for c in (1, 3):
                        act.wait_ge(sc_r, 4)
                        act.activation(g16[:, c, :, :], gf[:, c, :, :], ACT.Copy, scale=sc[:, 3, 3:4]).then_inc(n2a_r, 1)
                    for n, c in enumerate((0, 2)):
                        act.wait_ge(n3_r, n + 1)
                        act.activation(gf[:, c, :, :], g16[:, c, :, :], ACT.Copy, scale=sc[:, 4, 1:2]).then_inc(xo_r, 1)
            for b in range(B):
                act.wait_ge(ymm, b + 1)
                act.activation(yt[:, b, :, :], fbank[b][:, :], ACT.Tanh).then_inc(y_r, 1)

        @block.tensor
        def _(pe):
            def keys(layer):
                for g in range(G):
                    for part in range(2):
                        k = 2 * (G * layer + g) + part
                        if k >= len(kbank):
                            pe.wait_ge(kh_r, k - len(kbank) + 1)
                        pe.matmul(kbank[k % len(kbank)][:, 0:308], wkr_sb[:, layer, g, :],
                                  ctx_sb[:, 2 * part:2 * part + 2, :], start=True, stop=True).then_inc(kmm, 1)

            def values(layer):
                pe.wait_ge(tail_in, 16)
                pe.wait_ge(w_in if layer == 0 else wl_in, 16)
                for t in range(2):
                    for b in range(B):
                        keys = (ctx_sb[:, b, 0:P], tail_sb[:, b, :])[t]
                        ins = pe.matmul(pv[t][:, P * b:P * b + P], keys, weight(WL1 * layer + WV), start=True, stop=True)
                    ins.then_inc(vmm, 1)

            def turn_normed(kind, layer, b):
                k = norm_no[kind, layer, b]
                pe.wait_ge(xn_r, k + 1)
                fill_misc(pe, (kind, layer, b))
                for t in range(TT):
                    ins = pe.transpose(misc[:, P * t:P * t + P], xn[:, kind == "post", t, :], ident[:, :])
                ins.then_inc(misc_full, 1)

            def project_q(layer, b):
                pe.wait_ge(xnT_r, norm_no["pre", layer, b] + 1)
                fill_misc(pe, ("q", layer, b))
                pe.matmul(misc[:, :], weight(WL1 * layer + WQ), xnT[:, :], start=True, stop=True).then_inc(misc_full, 1)

            def scores_for_top(layer, b, u):
                n = B * layer + b
                k = units_before(n) + u
                if u == 0:
                    pe.wait_ge(q_in[n % 3], 3 * 16 * (n // 3 + 1))
                    pe.wait_ge(kd_r, n + 1)
                if k >= MRING:
                    pe.wait_ge(top_red, k - MRING + 1)
                qt, h0, heads, keys = UNITS[layer][u]
                masked = layer == 1 and qt < 2
                ps = top[k % MRING]
                g, j = h0 // J, h0 % J
                cols = ps[:, 0:keys * heads].rearrange("p (h k) -> p h k", h=heads)
                ins = pe.matmul(cols, Q4[n % 3][:, g, P * qt:P * qt + P], Kd[n % 2][:, g, j:j + heads, 0:keys],
                                start=True, stop=not masked, skip_group_check=True)
                if masked:
                    lo = 0 if qt == 0 else P
                    ins = pe.matmul(cols[:, :, lo:keys], identr[:, :],
                                    maskM[:, 0:keys - lo].unsqueeze(1).to_broadcast([P, heads, keys - lo]),
                                    start=False, stop=True, skip_group_check=True)
                ins.then_inc(top_r, 1)

            def turn_top(layer, b):
                n = B * layer + b
                pe.wait_ge(nms_r, n + 1)
                fill_misc(pe, ("top", layer, b))
                for t in range(TT):
                    ins = pe.transpose(misc[0:32, P * t:P * t + P],
                                       nms[:, t, :, :, :].rearrange("p a j g -> p (a j g)").bitcast(F32), ident[:, :])
                ins.then_inc(misc_full, 1)

            def scores(layer, b, t):
                n = B * layer + b
                k = TILES * n + t
                if t == 0:
                    pe.wait_ge(m_in[n % 3], 2 * 16 * (n // 3 + 1))
                if k >= SRING:
                    pe.wait_ge(exp_r, k - SRING + 1)
                ps = score[k % SRING]
                if t < H:
                    g, j = t % G, t // G
                    ins = pe.matmul(ps[:, :], K4[32 * j:32 * j + 32, g, b, 0:P],
                                    Q4[n % 3][32 * j:32 * j + 32, g, :], start=True, stop=(layer == 0),
                                    skip_group_check=True)
                    if layer == 1:
                        ins = pe.matmul(ps[:, 0:P], identr[:, :], maskT, start=False, stop=True, skip_group_check=True)
                else:
                    if t == H and b == 0:
                        pe.wait_ge(kt_r, layer + 1)
                    q0 = P if layer == 1 else 0
                    ins = pe.matmul(ps[:, q0:T], KT[:, b, t - H, :], Q4[n % 3][:, t - H, q0:T],
                                    start=True, stop=(layer == 0), skip_group_check=True)
                    if layer == 1:
                        ins = pe.matmul(ps[:, P:P + 32], identr[:, :], maskE, start=False, stop=True,
                                        skip_group_check=True)
                ins.then_inc(score_r, 1)

            def weigh(layer, b, r):
                n = B * layer + b
                if r == 0 and b == 0:
                    pe.wait_ge(v_r, layer + 1)
                if r in (0, 2) and n > 0:
                    pe.wait_ge(pvx, 2 * (n - 1) + r // 2 + 1)
                pe.wait_ge(exp_r, TILES * n + (4 * r + 4 if r < 4 else TILES))
                acc = pv[r // 2 if r < 4 else r - 4]
                q0 = P if layer == 1 and r >= 4 else 0
                for g in range(G):
                    if r < 4:
                        lhs, t = V4[:, b, g, r, :], 4 * r + g
                    else:
                        lhs, t = VT[:, b, g, 32 * (r - 4):32 * (r - 4) + 32], H + g
                    ins = pe.matmul(acc[32 * g:32 * g + 32, q0:T], lhs, pr[:, (TILES * n + t) % PRING, q0:T],
                                    start=(r in (0, 2)), stop=(r >= 4), skip_group_check=True)
                ins.then_inc(pv_r, 1)

            def project_out(layer, b):
                n = B * layer + b
                pe.wait_ge(oT_r, n + 1)
                fill_misc(pe, ("wo", layer, b))
                for t in range(TT):
                    ins = pe.matmul(misc[:, P * t:P * t + P], oT[:, P * t:P * t + P], weight(WL1 * layer + WO),
                                    start=True, stop=True)
                ins.then_inc(misc_full, 1)

            def step(b, k):
                if k == 0:
                    pe.wait_ge(xnT_r, norm_no["post", 1, b] + 1)
                    pe.wait_ge(c_r, b + 2)
                fill_misc(pe, (f"step{k}", 1, b))
                wx = (WF, WI, WC)[k]
                pe.matmul(misc[:, :], weight(wx), pnT[:, b, :], start=True, stop=False)
                pe.matmul(misc[:, :], weight(wx + 1), cst[:, :], start=False, stop=True).then_inc(misc_full, 1)

            def global_top(k):
                pe.wait_ge(amx_r, k + 1)
                fill_misc(pe, ("gt", k))
                pe.transpose(misc[0:1, 0:P], amx[:, k:k + 1], ident[:, :]).then_inc(misc_full, 1)
                pe.wait_ge(gtop_r, k + 1)
                fill_misc(pe, ("gb", k))
                pe.matmul(misc[:, 0:1], ones[0:1, :], gtop[0:1, k:k + 1], start=True, stop=True).then_inc(misc_full, 1)

            pe.wait_ge(k_in, 32)
            keys(0)
            pe.wait_ge(small_in, 48)
            turn_normed("pre", 0, 0)
            pe.wait_ge(w_in, 16)
            project_q(0, 0)
            values(0)
            for layer in range(2):
                for i in range(-1, B + 1):
                    for slot in range(SLOTS):
                        if 0 <= i < B and slot < TILES:
                            scores(layer, i, slot)
                        for b, u in units_at(layer, i, slot):
                            scores_for_top(layer, b, u)
                        for what, b in planned(PE_PLAN, layer, i, slot):
                            if what in ("pre", "post"):
                                turn_normed(what, layer, b)
                            elif what == "q":
                                project_q(layer, b)
                            elif what == "top":
                                turn_top(layer, b)
                            elif what == "wo":
                                project_out(layer, b)
                            elif what.startswith("round"):
                                weigh(layer, b, int(what[5]))
                            elif what.startswith("tail"):
                                weigh(layer, b, 4 + int(what[4]))
                            else:
                                step(b, int(what[4]))
                    if layer == 0 and i == -1:
                        pe.wait_ge(wq_r, 1)
                        for k in range(3):
                            fill_misc(pe, ("w", k))
                            for m in range(4 * k, min(4 * k + 4, 9)):
                                blk = wf_sb[:, 4 * m:4 * m + 4, :].rearrange("p a c -> p (a c)")
                                ins = pe.transpose(misc[:, P * (m % 4):P * (m % 4) + P], blk, ident[:, :])
                            ins.then_inc(misc_full, 1)
                if layer == 0:
                    pe.wait_ge(ones_r, 1)
                    pe.wait_ge(wT_r, 3)
                    pe.wait_ge(pvx, 2 * B)
                    pe.wait_ge(exp_r, TILES * B)
                    pe.wait_ge(top_red, units_before(B))
                    global_top(0)
                    for t in range(24):
                        c, m = t % 12 // 3, t % 3
                        if t < 12 and m == 0:
                            pe.wait_ge(xq_r, c + 1)
                        if t >= FRING:
                            pe.wait_ge(fev, t - FRING + 1)
                        pe.matmul(fbank[t % FRING][:, :], wfT[:, 3 * (t // 12) + m, :], xq[:, c, :],
                                  start=True, stop=True).then_inc(fmm, 1)
                        if t == 16:
                            global_top(1)
                    for k in range(2, 5):
                        if k == 3:
                            pe.wait_ge(fev, 24)
                            keys(1)
                            values(1)
                        global_top(k)
                    for c in range(B):
                        pe.wait_ge(xod_r if c % 2 else xo_r, c // 2 + 1)
                        if c == 0:
                            pe.wait_ge(kh_r, 4 * G)
                        for t in range(TT):
                            for m in range(NF):
                                ins = pe.matmul(fbank[c][:, P * t:P * t + P], gf[:, c, m, P * t:P * t + P],
                                                wfT[:, 6 + m, :], start=(t == 0 and m == 0), stop=(m == NF - 1),
                                                skip_group_check=True)
                        ins.then_inc(dmm, 1)
                        if c == 1:
                            turn_normed("pre", 1, 0)
                        if c == 2:
                            project_q(1, 0)
                    pe.wait_ge(x2_r, B)
                    pe.wait_ge(const_r, 2)
            pe.wait_ge(exp_r, 2 * TILES * B)
            pe.wait_ge(top_red, units_before(2 * B))
            for b in range(B):
                pe.matmul(fbank[b][:, :], ones[0:1, :], rows_sb[0:1, RFO:RFO + 1, :].to_broadcast([1, TT, C]),
                          start=True, stop=False, skip_group_check=True)
                for t in range(TT):
                    pe.matmul(fbank[b][:, P * t:P * t + P], pnT[:, b, P * t:P * t + P], weight(WOUT),
                              start=False, stop=False, skip_group_check=True)
            pe.wait_ge(c_r, B + 2)
            for b in range(B):
                for t in range(TT):
                    ins = pe.matmul(fbank[b][:, P * t:P * t + P], cst[:, P * t:P * t + P], weight(UOUT),
                                    start=False, stop=True, skip_group_check=True)
                ins.then_inc(ymm, 1)

        @block.vector
        def _(dve):
            chained = [0]
            chain = ctx.enter_context(nc.semaphore("chain"))

            def link(ins):
                chained[0] += 1
                ins.then_inc(chain, 1)
                dve.wait_ge(chain, chained[0])

            def keys():
                for g in range(G):
                    for part in range(2):
                        k = 2 * g + part
                        dve.wait_ge(kf_r, k + 1)
                        dve.wait_ge(kh_r, k + 1)
                        dst = K4[:, g, 2 * part:2 * part + 2, :].rearrange("p b s -> p (b s)")
                        dve.tensor_tensor(dst, kf[:, k % 2, :], kh[:, k % 2, :].bitcast(F32), ALU.subtract)\
                           .then_inc(k4_r, 1)
                        if k == 3:
                            norm("pre", 0, 0)

            def weights():
                dve.wait_ge(wf_in, 16)
                link(dve.tensor_reduce(wabs[:, 0, :], wf_sb[:, :, :], AX.X, ALU.max, apply_absolute_value=True))
                link(dve.tensor_scalar(wabs[:, 1, :], wabs[:, 0, :], 1.0 / WMAX, SMIN, ALU.mult, ALU.max))
                link(dve.reciprocal(wabs[:, 2, :], wabs[:, 1, :]))
                wide = [P, NBLK, 32]
                link(dve.tensor_tensor(wn16[:, :, :], wf_sb[:, :, :],
                                       wabs[:, 2, :].unsqueeze(2).to_broadcast(wide), ALU.mult))
                link(dve.tensor_scalar(wn16[:, :, :], wn16[:, :, :], WMAX, -WMAX - 1.0, ALU.min, ALU.max))
                dve.tensor_tensor(wf_sb[:, :, :], wn16[:, :, :],
                                  wabs[:, 1, :].unsqueeze(2).to_broadcast(wide), ALU.mult).then_inc(wq_r, 1)

            def norm_stats(kind, layer, b):
                k = norm_no[kind, layer, b]
                if (kind, layer) == ("pre", 0):
                    dve.wait_ge(x_in[b], 16)
                elif kind == "pre":
                    dve.wait_ge(x2_r, b + 1)
                else:
                    dve.wait_ge(res_r, B * layer + b + 1)
                for t in range(TT):
                    ins = dve.bn_stats(stat6[:, k % 4, t, :], xr[:, TT * b + t, :])
                link(ins)
                for t in range(TT):
                    ins = dve.bn_aggr(mv[:, k % 4, t, :], stat6[:, k % 4, t, :])
                ins.then_inc(mv_r, 1)

            def norm(kind, layer, b):
                k = norm_no[kind, layer, b]
                dve.wait_ge(mv_r, k + 1)
                dve.wait_ge(rstd_r, k + 1)
                if B * layer + b > 0:
                    dve.wait_ge(xnT_r, norm_no[kind, (B * layer + b - 1) // B, (b - 1) % B] + 1)
                for t in range(TT):
                    ins = dve.tensor_scalar(xn[:, kind == "post", t, :], xr[:, TT * b + t, :], mv[:, k % 4, t, 0:1],
                                            rstd[:, k % 4, t:t + 1], ALU.subtract, ALU.mult)
                ins.then_inc(xn_r, 1)

            def normed_max(b):
                dve.wait_ge(xn_r, norm_no["post", 0, b] + 1)
                dve.tensor_reduce(amax[:, 0, b:b + 1], xn[:, 1, :, :], AX.XY, ALU.max,
                                  apply_absolute_value=True).then_inc(am_r, 1)

            def q_low(layer, b):
                n = B * layer + b
                dve.wait_ge(qh_r, n + 1)
                if n >= 2:
                    dve.wait_ge(q_in[(n - 2) % 3], 3 * 16 * ((n - 2) // 3 + 1))
                dve.scalar_tensor_tensor(out=ql[:, n % 2, :], in0=misc[:, :],
                                         scalar=cols_sb[:, BQ + layer:BQ + layer + 1],
                                         in1=qh[:, n % 2, :].bitcast(F32), op0=ALU.add,
                                         op1=ALU.subtract).then_inc(ql_r, 1)

            def take_top(layer, b, u):
                k = units_before(B * layer + b) + u
                qt, h0, heads, keys = UNITS[layer][u]
                dve.wait_ge(top_r, k + 1)
                dve.tensor_reduce(nm[:, qt, h0:h0 + heads],
                                  top[k % MRING][:, 0:keys * heads].rearrange("p (h k) -> p h k", h=heads),
                                  AX.X, ALU.max, negate=True).then_inc(top_red, 1)

            def split_top(layer, b):
                n = B * layer + b
                dve.wait_ge(top_red, units_before(n + 1))
                src = nm[:, :, :].rearrange("p t (g j) -> p t j g", g=G)
                part = [nms[:, :, a, :, :] for a in range(2)]
                if n > 0:
                    dve.wait_ge(nmT_r, n)
                dve.tensor_copy(part[0], src).then_inc(nmh_r, 1)
                dve.wait_ge(nmh_r, n + 1)
                dve.tensor_tensor(part[1], src, part[0].bitcast(F32), ALU.subtract).then_inc(nms_r, 1)

            def divide(layer, b, part):
                n = B * layer + b
                if part < 2:
                    dve.wait_ge(pv_r, ROUNDS * n + 5 + part)
                    dve.transpose(oq[:, part, :, :, :].rearrange("p k e r -> p (k e r)"), pv[part][:, :]).then_inc(pvx, 1)
                elif part == 2:
                    dve.wait_ge(pvx, 2 * n + 2)
                    link(dve.reciprocal(orc[:, :, :, :].rearrange("p a k e -> p (a k) e"),
                                        oq[:, :, :, :, D].rearrange("p a k e -> p (a k) e")))
                    for a in range(2):
                        ins = dve.tensor_tensor(oc[:, :, a, :, :], oq[:, a, :, :, 0:D],
                                                orc[:, a, :, :].unsqueeze(3).to_broadcast([P, T // 32, 2, D]), ALU.mult)
                    ins.then_inc(oc_r, 1)
                else:
                    dve.wait_ge(oc_r, n + 1)
                    if n > 0:
                        dve.wait_ge(misc_full, use["wo", (n - 1) // B, (n - 1) % B] + 1)
                    dve.transpose(oT[:, :], oc[:, :, :, :, :].rearrange("p k a e d -> p (k a e d)")).then_inc(oT_r, 1)

            def residual(layer, b):
                n = B * layer + b
                dve.wait_ge(misc_full, use["wo", layer, b] + 1)
                dve.wait_ge(xg_r, n + 1)
                dve.scalar_tensor_tensor(out=xr[:, TT * b:TT * b + TT, :].rearrange("p t c -> p (t c)"),
                                         in0=misc[:, :], scalar=tg[:, layer:layer + 1],
                                         in1=xg[:, n % 2, :, :].rearrange("p t c -> p (t c)"),
                                         op0=ALU.mult, op1=ALU.add).then_inc(res_r, 1)

            def update(b):
                if b == 0:
                    dve.wait_ge(v_r, 2)
                dve.wait_ge(gt_r, 3 * b + 1)
                dve.scalar_tensor_tensor(out=tmp[:, 0, :], in0=gt[:, 0, :], scalar=1.0, in1=cst[:, :],
                                         op0=ALU.add, op1=ALU.mult).then_inc(ct_r, 1)
                dve.wait_ge(gt_r, 3 * b + 3)
                dve.scalar_tensor_tensor(out=tmp[:, 1, :], in0=gt[:, 1, :], scalar=1.0, in1=gt[:, 2, :],
                                         op0=ALU.add, op1=ALU.mult).then_inc(ct_r, 1)
                dve.wait_ge(ct_r, 2 * b + 2)
                dve.scalar_tensor_tensor(out=cst[:, :], in0=tmp[:, 0, :], scalar=0.5, in1=tmp[:, 1, :],
                                         op0=ALU.mult, op1=ALU.add).then_inc(c_r, 1)

            def part_max(k, n_parts):
                dve.wait_ge(am_r, am_count[k])
                dve.tensor_reduce(amx[:, k:k + 1], amax[:, k, 0:n_parts], AX.X, ALU.max).then_inc(amx_r, 1)

            def full_max(k):
                dve.wait_ge(misc_full, use["gt", k] + 1)
                dve.tensor_reduce(gtop[0:1, k:k + 1], misc[0:1, 0:P], AX.X, ALU.max).then_inc(gtop_r, 1)

            def factors(src, to, constant, aps):
                while True:
                    first, second = constant, aps[0] if aps else None
                    constant, aps = (aps[1] if len(aps) > 1 else None), aps[2:]
                    ins = dve.tensor_scalar(to, src, first, second, ALU.mult, *((ALU.mult,) if second is not None else ()))
                    if constant is None:
                        return ins
                    link(ins)
                    src = to

            def scale_of(k, raw=1.0, aps=()):
                dve.wait_ge(gtop_r, k + 1)
                dve.wait_ge(misc_full, use["gb", k] + 1)
                factors(misc[:, 0:1], sc[:, k, 0:1], raw, aps).then_inc(smax_r, 1)
                dve.wait_ge(smax_r, k + 1)
                link(dve.tensor_scalar(sc[:, k, 1:2], sc[:, k, 0:1], 1.0 / QMAX, SMIN, ALU.mult, ALU.max))
                link(dve.reciprocal(sc[:, k, 2:3], sc[:, k, 1:2]))
                src, constant = (sc[:, k, 1:2], 0.5) if k == 1 else (sc[:, k, 2:3], raw)
                factors(src, sc[:, k, 3:4], constant, aps).then_inc(sc_r, 1)
                dve.wait_ge(sc_r, k + 1)

            def ffn():
                flat = lambda t, c: t[:, c, :, :].rearrange("p m t -> p (m t)")

                def whole_max(k, c, src):
                    dve.tensor_reduce(amax[:, k, c:c + 1], flat(src, c), AX.X, ALU.max,
                                      apply_absolute_value=True).then_inc(am_r, 1)

                def absmax(k, t, src):
                    dve.wait_ge(fev, t + 1)
                    dve.tensor_reduce(amax[:, k, t % 12:t % 12 + 1], src[:, t % 12 // 3, t % 3, :], AX.X, ALU.max,
                                      apply_absolute_value=True).then_inc(am_r, 1)

                part_max(0, B)
                full_max(0)
                scale_of(0)
                for c in range(B):
                    dve.wait_ge(xnT_r, norm_no["post", 0, B - 1] + 1)
                    dve.tensor_scalar(n16[:, c, :], pnT[:, c, :], sc[:, 0, 2:3], None, ALU.mult).then_inc(n16_r, 1)
                    dve.wait_ge(n16_r, c + 1)
                    dve.tensor_scalar(xq[:, c, :], n16[:, c, :], sc[:, 0, 1:2], None, ALU.mult).then_inc(xq_r, 1)

                for t in range(12):
                    absmax(1, t, gf)
                part_max(1, 12)
                full_max(1)
                scale_of(1)
                for c in range(B):
                    dve.tensor_scalar(flat(g16, c), flat(gf, c), sc[:, 1, 2:3], None, ALU.mult).then_inc(g16_r, 1)
                    for t in range(12 + 3 * c, 15 + 3 * c):
                        absmax(2, t, uf)
                part_max(2, 12)
                for c in range(B):
                    if c % 2 == 0:
                        dve.wait_ge(th_r, c + 1)
                        dve.tensor_scalar(flat(s16, c), flat(gf, c), 32768.0, 32768.0, ALU.mult, ALU.add).then_inc(s16_r, 1)
                        dve.wait_ge(s16_r, c // 2 + 1)
                    else:
                        dve.wait_ge(s16a_r, c // 2 + 1)
                    dve.wait_ge(g16_r, c + 1)
                    dve.tensor_tensor(flat(gf, c), flat(g16, c), flat(s16, c), ALU.mult).then_inc(g2_r, 1)
                    dve.wait_ge(g2_r, c + 1)
                    whole_max(3, c, gf)
                    if c == 0:
                        full_max(2)
                    if c == 1:
                        scale_of(2)
                part_max(3, B)
                full_max(3)
                scale_of(3, 2.0 ** -16, (sc[:, 1, 1:2],))
                for c in range(B):
                    if c % 2 == 0:
                        dve.tensor_scalar(flat(g16, c), flat(gf, c), sc[:, 3, 3:4], None, ALU.mult).then_inc(n2_r, 1)
                        dve.wait_ge(n2_r, c // 2 + 1)
                    else:
                        dve.wait_ge(n2a_r, c // 2 + 1)
                    dve.wait_ge(u16_r, c + 1)
                    dve.tensor_tensor(flat(uf, c), flat(g16, c), flat(u16, c), ALU.mult).then_inc(o_r, 1)
                    dve.wait_ge(o_r, c + 1)
                    whole_max(4, c, uf)
                part_max(4, B)
                full_max(4)
                scale_of(4, 1.0, (sc[:, 3, 1:2], sc[:, 2, 1:2]))
                for n, c in enumerate((0, 2, 1, 3)):
                    dve.tensor_scalar(flat(g16, c), flat(uf, c), sc[:, 4, 3:4], None, ALU.mult).then_inc(n3_r, 1)
                    if n >= 2:
                        dve.wait_ge(n3_r, n + 1)
                        dve.tensor_scalar(flat(gf, c), flat(g16, c), sc[:, 4, 1:2], None, ALU.mult).then_inc(xod_r, 1)
                for c in range(B):
                    dve.wait_ge(dmm, c + 1)
                    xc = xr[:, TT * c:TT * c + TT, :].rearrange("p t c -> p (t c)")
                    dve.scalar_tensor_tensor(out=xc, in0=fbank[c][:, :], scalar=tg[:, 2:3], in1=xc,
                                             op0=ALU.mult, op1=ALU.add).then_inc(x2_r, 1)
                    if c < 2:
                        norm_stats("pre", 1, c)
                    if c == 0:
                        norm("pre", 1, 0)
                q_low(1, 0)

            am_count = {0: 4, 1: 16, 2: 28, 3: 32, 4: 36}

            dve.memset(ones[:, :], 1.0).then_inc(ones_r, 1)
            dve.memset(Q4[0][:, :, :].bitcast(F32), 0.0).then_inc(q4_clear, 1)
            dve.wait_ge(ones_r, 1)
            norm_stats("pre", 0, 0)
            dve.wait_ge(small_in, 48)
            dve.tensor_scalar(lcols[:, :], cols_sb[:, BK:BK + 2 * G], lowrow, None, ALU.mult).then_inc(lcol_r, 1)
            dve.wait_ge(gates, 1)
            for n in range(2):
                dve.tensor_scalar(bog[:, n, :], rows_sb[:, RO + n, :], tg[:, n:n + 1], None, ALU.mult).then_inc(bias_r, 1)
            for n in range(2):
                dve.tensor_scalar(bvt[:, n, :], rows_sb[:, RV + n, :], own[:, 0:1], None, ALU.mult).then_inc(bias_r, 1)
            norm_stats("pre", 0, 1)
            keys()
            q_low(0, 0)
            weights()

            for layer in range(2):
                for i in range(-1, B + 1):
                    for slot in range(SLOTS):
                        for b, u in units_at(layer, i, slot):
                            take_top(layer, b, u)
                        for what, b in planned(DVE_PLAN, layer, i, slot):
                            if what.startswith("stat"):
                                if what != "stat pre" or b > 1:
                                    norm_stats(what[5:], layer, b)
                            elif what.startswith("div"):
                                divide(layer, b, int(what[3]))
                            elif what == "wo":
                                residual(layer, b)
                            elif what in ("pre", "post"):
                                norm(what, layer, b)
                            elif what == "amax":
                                normed_max(b)
                            elif what == "q":
                                q_low(layer, b)
                            elif what == "top":
                                split_top(layer, b)
                            else:
                                update(b)
                    if layer == 0 and i == -1:
                        dve.tensor_scalar(cst[:, :].rearrange("p (t c) -> p t c", c=P),
                                          ones[:, :].unsqueeze(1).to_broadcast([P, TT, P]),
                                          cols_sb[:, INC:INC + 1], 2.0, ALU.mult, ALU.mult).then_inc(c_r, 1)
                        dve.wait_ge(wl_in, 16)
                        for wu in (UF, UI, UC, UOUT):
                            ins = dve.tensor_scalar(wsb[:, wu, :], wsb[:, wu, :], 0.5, None, ALU.mult)
                        ins.then_inc(c_r, 1)
                if layer == 0:
                    ffn()
            for b in range(B):
                dve.wait_ge(y_r, b + 1)
                yb = yt[:, b, :, :].rearrange("p t c -> p (t c)")
                xb = xr[:, TT * b:TT * b + TT, :].rearrange("p t c -> p (t c)")
                dve.scalar_tensor_tensor(out=xb, in0=yb, scalar=tg[:, 3:4], in1=xb,
                                         op0=ALU.mult, op1=ALU.add).then_inc(out_r, 1)


_WEIGHTS = ["L0_xattn_Wq", "L0_xattn_Wv", "L0_xattn_Wo", "L1_xattn_Wq", "L1_xattn_Wv", "L1_xattn_Wo",
            "L1_ffn_wf", "L1_ffn_uf", "L1_ffn_wi", "L1_ffn_ui", "L1_ffn_wc", "L1_ffn_uc", "L1_ffn_wo",
            "L1_ffn_uo"]


def constants():
    a = np.arange(P)
    ident = np.eye(P)
    top = np.where(a[None, :] > a[:, None], NEG, 0.0)
    main = np.where(a[:, None] > a[None, :], NEG, 0.0)
    tail = np.where((a % 32)[:, None] > np.arange(32)[None, :] + OWN, NEG, 0.0)
    own = (a % 32 >= OWN)[:, None]
    low = (a % PARTS == 2)[:, None]
    key = (a % PARTS < 3)[:, None]
    return np.concatenate([ident, top, main, tail, own, low, key], axis=1).astype(np.float32)


def kernel(**inputs):
    import concourse.bacc as bacc
    from concourse.bass_utils import run_bass_kernel_spmd

    order = np.arange(C).reshape(G, J, D).transpose(1, 2, 0).reshape(-1)
    turned = []
    for name in _WEIGHTS:
        t = np.asarray(inputs[name]).T
        turned.append(t[:, order] if name.endswith("Wq") else t)
    wkr = np.zeros((C, 2, G, J, 32), np.float32)
    bkr = np.ones((J, 32, 2, G), np.float32)
    for n in range(2):
        wk = np.asarray(inputs[f"L{n}_xattn_Wk"]).T.reshape(C, G, J, D)
        bk = np.asarray(inputs[f"L{n}_xattn_bk"]).reshape(G, J, D)
        for part in range(3):
            wkr[:, n, :, :, part::PARTS] = wk
            bkr[:, part::PARTS, n, :] = bk.transpose(1, 2, 0)
    ctx = np.asarray(inputs["ctx_1024"]).transpose(2, 0, 1)
    tail = np.zeros((C, B, 4, 32), np.float32)
    tail[:, :, :, OWN:] = ctx[:, :, None, P:]
    wffn = [np.asarray(inputs[f"L0_ffn_w_{n}"]).reshape(NF, P, C).transpose(1, 0, 2).reshape(P, -1) for n in ("gate", "up")]
    wffn.append(np.asarray(inputs["L0_ffn_w_down"]))
    cols = [np.asarray(inputs[f"{n}"])[order] for n in ("L0_xattn_bq", "L1_xattn_bq")]
    cols += [np.asarray(inputs[f"L1_ffn_{n}"]) for n in ("bf", "bi", "bc", "in_c")]
    gates = np.zeros(C, np.float32)
    gates[0:2], gates[2:4] = inputs["g_xattn"], inputs["g_ffn"]
    rows = [np.asarray(inputs[n]) for n in ("L0_xattn_bv", "L1_xattn_bv", "L0_xattn_bo", "L1_xattn_bo", "L1_ffn_bo")]
    arrays = {
        "x": np.asarray(inputs["x"]),
        "w": np.stack(turned, axis=1),
        "wkr": wkr.reshape(C, 2, G, P),
        "ctxT": ctx,
        "tailT": tail.reshape(C, B, P),
        "wffn": np.concatenate(wffn, axis=1).reshape(P, NBLK, 32),
        "cols": np.concatenate([np.stack(cols, axis=1), bkr.reshape(P, 2 * G)], axis=1),
        "rows": np.stack(rows + [gates], axis=0),
        "consts": constants(),
    }
    arrays = {k: np.ascontiguousarray(v) for k, v in arrays.items()}
    nc = bacc.Bacc("TRN2", target_bir_lowering=False, num_devices=1)
    args = [nc.dram_tensor(k, v.shape, F32, kind="ExternalInput").ap() for k, v in arrays.items()]
    out = nc.dram_tensor("out", (B, T, C), F32, kind="ExternalOutput").ap()
    program(nc, *args, out)
    result = run_bass_kernel_spmd(nc, [arrays], core_ids=[0])
    return result.results[0]["out"]
```

```python
from contextlib import ExitStack

import numpy as np

import concourse.bass as bass
from concourse import mybir

F32 = mybir.dt.float32
F32R = mybir.dt.float32r
I16 = mybir.dt.int16
U16 = mybir.dt.uint16
ALU = mybir.AluOpType
ACT = mybir.ActivationFunctionType
AX = mybir.AxisListType

P = 128
B, T, C = 4, 512, 128
TT = T // P
S = 154
H, D = 16, 8
G, J = 4, 4
NF = 3
TAIL0 = S - 32
OWN = P - TAIL0
SCALE = float(D) ** -0.5
EPS = 1e-5
NEG = -2.0 ** 126
QMAX = 32767.0
WMAX = 7.0
SMIN = 1e-12
NBLK = 36

PARTS = 4

SLOTS = 20
TILES = H + G
ROUNDS = 6
EARLY, LAST = 3, 13
PRING = 8
SRING = 2
MRING = 3
FRING = SRING + MRING + 2

WQ, WV, WO = 0, 1, 2
WL1 = 3
WF, UF, WI, UI, WC, UC, WOUT, UOUT = range(6, 14)
NW = 14
BQ, BF, BI, BC, INC, BK = 0, 2, 3, 4, 5, 6
NCOL = BK + 2 * G
RV, RO, RFO, RG = 0, 2, 4, 5


def max_units(layer):
    units = []
    for qt in range(TT):
        heads, keys = (J, P) if layer == 1 and qt == 0 else (J // 2, S)
        units += [(qt, h, heads, keys) for h in range(0, H, heads)]
    return units


UNITS = [max_units(0), max_units(1)]


def units_at(layer, i, slot):
    n = len(UNITS[layer])
    share = lambda k: range(n * k // (EARLY + LAST), n * (k + 1) // (EARLY + LAST))
    taken = []
    if slot < LAST and 0 <= i + 1 < B:
        first = 0 if (i, slot) == (-1, 0) else slot + EARLY
        taken += [(i + 1, u) for k in range(first, slot + EARLY + 1) for u in share(k)]
    if slot >= SLOTS - EARLY and i + 2 < B:
        taken += [(i + 2, u) for u in share(slot - SLOTS + EARLY)]
    return taken


def units_before(n):
    return sum(len(UNITS[m // B]) for m in range(n))


PE_PLAN = [(1, "tail0", -1), (3, "tail1", -1), (4, "pre", 2), (6, "q", 2), (7, "round0", 0), (8, "wo", -1),
           (10, "round1", 0), (13, "round2", 0), (14, "top", 1), (16, "post", -1), (17, "round3", 0),
           (4, "state0", "first"), (4, "step0", "first"), (6, "state1", "first"), (6, "step1", "first"),
           (8, "state2", "first"), (8, "step2", "first"),
           (16, "state0", "second"), (17, "step0", "second"), (17, "state1", "second"), (18, "step1", "second"),
           (18, "state2", "second"), (19, "step2", "second")]
ACT_PLAN = [(5, "pre", 2), (6, "q", 2), (14, "top", 1), (16, "post", -1),
            (5, "step0", "first"), (7, "step1", "first"), (9, "step2", "first"),
            (17, "step0", "second"), (18, "step1", "second"), (19, "step2", "second")]
DVE_PLAN = [(0, "stat pre", 2), (3, "pre", 2), (3, "div0", -1), (3, "div1", -1), (5, "div2", -1), (6, "div3", -1),
            (7, "q", 2), (8, "wo", -1), (9, "stat post", -1), (13, "top", 1), (14, "post", -1), (16, "amax", -1),
            (10, "step", "first"), (19, "step", "second")]
STEPS = {(3, "first"): 0, (3, "second"): 1, (4, "first"): 2, (4, "second"): 3}
MISC_USERS = ("wo", "pre", "q", "post", "top")

WEIGHTS_AT = (0, B, 3)


def ahead(layer):
    return 1 + layer


def planned(plan, layer, i, slot):
    for at, what, shift in plan:
        if at != slot:
            continue
        if what.startswith(("step", "state")):
            if layer == 1 and (i, shift) in STEPS:
                yield what, STEPS[i, shift]
        elif i + shift in range(ahead(layer) if shift == 2 else 0, B) and (layer == 0 or what != "amax"):
            yield what, i + shift


def norm_order():
    order = []
    for layer in range(2):
        for i in range(-2, B + 1):
            order += [(kind, layer, b) for kind, b in (("pre", i + 2), ("post", i - 1)) if 0 <= b < B]
    return order


NORMS = norm_order()
norm_no = {name: k for k, name in enumerate(NORMS)}


def misc_plan():
    order = []
    for layer in range(2):
        order += [(what, layer, b) for b in range(ahead(layer)) for what in ("pre", "q")]
        for i in range(-1, B + 1):
            for slot in range(SLOTS):
                order += [(what, layer, b) for what, b in planned(PE_PLAN, layer, i, slot) if what in MISC_USERS]
                if (layer, i, slot) == WEIGHTS_AT:
                    order += [("w", 0), ("w", 1), ("w", 2)]
        if layer == 0:
            for k in range(5):
                order += [("gt", k), ("gb", k)]
    return order


def program(nc, x, w, wkr, ctxT, tailT, wffn, cols, rows, consts, masks, out):
    with ExitStack() as ctx:
        def sb(name, shape, dt=F32):
            return ctx.enter_context(nc.sbuf_tensor("sb_" + name, shape, dt))

        def bank(name):
            return ctx.enter_context(nc.psum_tensor("ps_" + name, [P, 512], F32))

        def sem(name):
            return ctx.enter_context(nc.semaphore(name))

        xr = sb("xr", [P, B * TT, C])
        wsb = sb("wsb", [P, NW, C])
        ctx_sb = sb("ctx", [P, B, S])
        tail_sb = sb("tail", [P, B, P])
        wf_sb = sb("wf", [P, NBLK, 32])
        wabs = sb("wabs", [P, 3, NBLK])
        wkr_sb = sb("wkr", [P, 2, G, P])
        wfT = sb("wfT", [P, 9, C])
        cols_sb = sb("cols", [P, NCOL])
        lcols = sb("lcols", [P, 2 * G])
        hcols = sb("hcols", [P, NCOL])
        rows_sb = sb("rows", [P, 6, C])
        tg = sb("tg", [P, 4])
        bog = sb("bog", [P, 2, C])
        bvt = sb("bvt", [P, 2, C])
        consts_sb = sb("consts", [P, P + 3])
        ident = consts_sb[:, 0:P]
        own = consts_sb[:, P:P + 1]
        lowrow = consts_sb[:, P + 1:P + 2]
        keyrow = consts_sb[:, P + 2:P + 3]
        cmask = sb("cmask", [P, 2 * P + 32])
        identr = sb("identr", [P, P], F32R)
        maskr = sb("maskr", [P, 2 * P + 32], F32R)
        maskM, maskT, maskE = maskr[:, 0:P], maskr[:, P:2 * P], maskr[:, 2 * P:2 * P + 32]
        ones = sb("ones", [P, P])
        onesr = sb("onesr", [1, P], F32R)
        bfo = sb("bfo", [1, 2, C], F32R)
        stat6 = sb("stat6", [P, 4, TT, 6])
        mv = sb("mv", [P, 4, TT, 2])
        var = sb("var", [P, 4, TT])
        half = sb("half", [P, TT])
        rstd = sb("rstd", [P, 4, TT])
        xn = sb("xn", [P, 2, TT, C])
        pnT = sb("pnT", [P, B, T])
        K4 = sb("K4", [P, G, B, S], F32R)
        KT = sb("KT", [P, B, G, P], F32R)
        V4 = sb("V4", [P, B, G, J, 32])
        VT = sb("VT", [P, B, G, 64])
        kf = sb("kf", [P, 2, 2 * S])
        kh = sb("kh", [P, 2, 2 * S], F32R)
        tmp = sb("tmp", [P, 2, T])
        vf = tmp
        nm = sb("nm", [P, TT, H])
        nms = sb("nms", [P, TT, 2, J, G], F32R)
        orc = sb("orc", [P, 2, T // 32, 2])
        amax = sb("amax", [P, 5, 12])
        amx = sb("amx", [P, 5])
        gtop = sb("gtop", [1, 5])
        sc = sb("sc", [P, 5, 4])
        cst = sb("cst", [P, T])

        with ExitStack() as stretch:
            def sb_here(name, shape, dt=F32):
                return stretch.enter_context(nc.sbuf_tensor("sb_" + name, shape, dt))

            Q4 = [sb_here(f"Q4{n}", [P, G, T], F32R) for n in range(3)]
            Kd = [sb_here(f"Kd{n}", [P, G, J, S], F32R) for n in range(2)]
            qh = sb_here("qh", [P, 2, T], F32R)
            pr = sb_here("pr", [P, PRING, T])
            oq = sb_here("oq", [P, 2, T // 32, 2, 16])
            oc = sb_here("oc", [P, T // 32, 2, 2, D])
            oT = sb_here("oT", [P, T])
            gt = sb_here("gt", [P, 3, T])
            wn16 = gt[:, :, :].rearrange("p k t -> p (k t)").bitcast(I16)[:, 0:NBLK * 32].rearrange("p (n c) -> p n c", c=32)
            yt = pr[:, 0:B, :].rearrange("p b (t c) -> p b t c", c=C)
            ql = sb_here("ql", [P, 2, T], F32R)
            nmT = sb_here("nmT", [32, 2, T], F32R)
            xnT = sb_here("xnT", [P, T])
            xg = sb_here("xg", [P, 2, TT, C])
        with ExitStack() as stretch:
            def sb_here(name, shape, dt=F32):
                return stretch.enter_context(nc.sbuf_tensor("sb_" + name, shape, dt))

            s16 = sb_here("s16", [P, B, NF, T], U16)
            u16 = sb_here("u16", [P, B, NF, T], I16)
            uf = sb_here("uf", [P, B, NF, T])
            gf = sb_here("gf", [P, B, NF, T])
            g16 = sb_here("g16", [P, B, NF, T], I16)
            n16 = sb_here("n16", [P, B, T], I16)
            xq = sb_here("xq", [P, B, T])

        score = [bank(f"score{n}") for n in range(SRING)]
        top = [bank(f"top{n}") for n in range(MRING)]
        pv = [bank(f"pv{n}") for n in range(2)]
        misc = bank("misc")
        fbank = score + top + pv
        ybank = score + pv
        kbank = score + top

        x_in = [sem(f"x_in{b}") for b in range(B)]
        w_in, small_in, k_in, tail_in, wl_in, wf_in, mask_in = (
            sem(n) for n in ("w_in", "small_in", "k_in", "tail_in", "wl_in", "wf_in", "mask_in"))
        const_r = sem("const_r")
        gates = sem("gates")
        lcol_r = sem("lcol_r")
        bias_r = sem("bias_r")
        ones_r, half_r = sem("ones_r"), sem("half_r")
        bfo_r = sem("bfo_r")
        q4_clear, kd_clear = sem("q4_clear"), sem("kd_clear")
        zero_r = sem("zero_r")
        misc_full = sem("misc_full")
        kmm, vmm = sem("kmm"), sem("vmm")
        kf_r, kh_r, k4_r = sem("kf_r"), sem("kh_r"), sem("k4_r")
        kd_r = sem("kd_r")
        kt_r = sem("kt_r")
        v_r, vf_r = sem("v_r"), sem("vf_r")
        mv_r, var_r, rstd_r = sem("mv_r"), sem("var_r"), sem("rstd_r")
        xn_r, xnT_r = sem("xn_r"), sem("xnT_r")
        qh_r, ql_r = sem("qh_r"), sem("ql_r")
        q_in = [sem(f"q_in{n}") for n in range(3)]
        m_in = [sem(f"m_in{n}") for n in range(3)]
        top_r, top_red = sem("top_r"), sem("top_red")
        nmh_r, nms_r, nmT_r = sem("nmh_r"), sem("nms_r"), sem("nmT_r")
        score_r, exp_r, pv_r = sem("score_r"), sem("exp_r"), sem("pv_r")
        pvx = sem("pvx")
        oc_r, oT_r = sem("oc_r"), sem("oT_r")
        xg_r, res_r = sem("xg_r"), sem("res_r")
        wq_r, wT_r = sem("wq_r"), sem("wT_r")
        fmm, fev = sem("fmm"), sem("fev")
        am_r, amx_r, gtop_r, sc_r = sem("am_r"), sem("amx_r"), sem("gtop_r"), sem("sc_r")
        xq_r, g16_r, th_r, s16_r, g2_r, n2_r, u16_r, o_r, n3_r, xo_r = (
            sem(n) for n in ("xq_r", "g16_r", "th_r", "s16_r", "g2_r", "n2_r", "u16_r", "o_r", "n3_r", "xo_r"))
        n16_r, smax_r = sem("n16_r"), sem("smax_r")
        s16a_r, n2a_r = sem("s16a_r"), sem("n2a_r")
        xod_r = sem("xod_r")
        dmm, x2_r = sem("dmm"), sem("x2_r")
        gmm = sem("gmm")
        gt_r, ct_r, c_r = sem("gt_r"), sem("ct_r"), sem("c_r")
        ymm, y_r = sem("ymm"), sem("y_r")
        out_r, out_in = sem("out_r"), sem("out_in")

        misc_uses = misc_plan()
        use = {name: n for n, name in enumerate(misc_uses)}

        def misc_read(name):
            kind = name[0]
            if kind in ("pre", "post"):
                return xnT_r, norm_no[name] + 1
            if kind == "q":
                return ql_r, B * name[1] + name[2] + 1
            if kind == "top":
                return nmT_r, B * name[1] + name[2] + 1
            if kind == "wo":
                return res_r, B * name[1] + name[2] + 1
            if kind == "w":
                return wT_r, name[1] + 1
            return (gtop_r if kind == "gt" else smax_r), name[1] + 1

        block = ctx.enter_context(nc.Block())

        def fill_misc(pe, name):
            if use[name] > 0:
                pe.wait_ge(*misc_read(misc_uses[use[name] - 1]))

        def weight(n):
            return wsb[:, n, :]

        @block.sync
        def _(sp):
            xd = x.rearrange("b (t p) c -> p b t c", p=P)
            sp.dma_start(xr[:, 0:TT, :], xd[:, 0]).then_inc(x_in[0], 16)
            sp.dma_start(wsb[:, 0:WL1, :], w[:, 0:WL1, :]).then_inc(w_in, 16)
            sp.dma_start(ctx_sb[:, :, :], ctxT).then_inc(k_in, 16)
            sp.dma_start(wkr_sb[:, 0, :, :], wkr[:, 0]).then_inc(k_in, 16)
            sp.dma_start(tail_sb[:, :, :], tailT).then_inc(tail_in, 16)
            for b in range(1, B):
                sp.dma_start(xr[:, TT * b:TT * b + TT, :], xd[:, b]).then_inc(x_in[b], 16)
            sp.dma_start(wf_sb[:, :, :], wffn).then_inc(wf_in, 16)
            sp.dma_start(wsb[:, WL1:NW, :], w[:, WL1:NW, :]).then_inc(wl_in, 16)
            sp.dma_start(wkr_sb[:, 1, :, :], wkr[:, 1]).then_inc(wl_in, 16)
            sp.dma_start(cmask[:, :], masks).then_inc(mask_in, 16)

            def queries(layer, b):
                n = B * layer + b
                sp.wait_ge(q4_clear, 3 * layer + min(b, 2) + 1)
                if n >= 3:
                    sp.wait_ge(score_r, TILES * (n - 2))
                for a, (src, ready) in enumerate(((qh, qh_r), (ql, ql_r), (qh, qh_r))):
                    sp.wait_ge(ready, n + 1)
                    sp.dma_start(Q4[n % 3][a:P:PARTS, :, :].bitcast(F32),
                                 src[:, n % 2, :].bitcast(F32)).then_inc(q_in[n % 3], 16)

            def tops(layer, b):
                n = B * layer + b
                sp.wait_ge(nmT_r, n + 1)
                for a in range(2):
                    sp.dma_start(Q4[n % 3][3 + PARTS * a:P:32, :, :].bitcast(F32),
                                 nmT[16 * a:16 * a + 16, n % 2, :].bitcast(F32)).then_inc(m_in[n % 3], 16)

            for layer in range(2):
                for b in range(ahead(layer)):
                    queries(layer, b)
                for i in range(-1, B + 1):
                    if ahead(layer) <= i + 2 < B:
                        queries(layer, i + 2)
                    if 0 <= i + 1 < B:
                        tops(layer, i + 1)
            od = out.rearrange("b (t p) c -> p b t c", p=P)
            for b in range(B):
                sp.wait_ge(out_r, b + 1)
                sp.dma_start(od[:, b], xr[:, TT * b:TT * b + TT, :]).then_inc(out_in, 16)
            sp.wait_ge(out_in, 16 * B)

        @block.gpsimd
        def _(pool):
            chained = [0]
            chain = ctx.enter_context(nc.semaphore("pool_chain"))

            def link(ins):
                chained[0] += 1
                ins.then_inc(chain, 1)
                pool.wait_ge(chain, chained[0])

            pool.memset(half[:, :], -0.5).then_inc(half_r, 1)

            def clear(layer):
                if layer == 1:
                    pool.wait_ge(o_r, B)
                    for b in range(3):
                        pool.memset(Q4[(B + b) % 3][:, :, :].bitcast(F32), 0.0).then_inc(q4_clear, 1)
                    pool.wait_ge(n3_r, B)
                for n in range(2):
                    pool.memset(Kd[n][:, :, :, :].bitcast(F32), 0.0).then_inc(kd_clear, 1)

            def keys_late():
                for g in range(G):
                    for part in range(2):
                        k = 2 * (G + g) + part
                        pool.wait_ge(kf_r, k - 2 * G + 1)
                        pool.wait_ge(kh_r, k + 1)
                        if k == 2 * G:
                            pool.wait_ge(score_r, TILES * B)
                        dst = K4[:, g, 2 * part:2 * part + 2, :].rearrange("p b s -> p (b s)")
                        pool.tensor_tensor(dst, kf[:, k % 2, :], kh[:, k % 2, :].bitcast(F32), ALU.subtract)\
                            .then_inc(k4_r, 1)

            def diagonal(layer, b):
                n = B * layer + b
                pool.wait_ge(top_r, units_before(n - 1))
                for j in range(J):
                    q = slice(32 * j, 32 * j + 32)
                    ins = pool.tensor_scalar(Kd[n % 2][q, :, j, :], K4[q, :, b, :].bitcast(F32), keyrow[q, 0:1], 1.0,
                                             ALU.mult, ALU.mult)
                    if j < J - 1:
                        link(ins)
                ins.then_inc(kd_r, 1)
                pool.wait_ge(kd_r, n + 1)

            def tail_keys(layer):
                pool.wait_ge(k4_r, 8 * layer + 8)
                for j in range(J):
                    q = slice(32 * j, 32 * j + 32)
                    ins = pool.tensor_copy(KT[q, :, :, 32 * j:32 * j + 32],
                                           K4[q, :, :, TAIL0:S].rearrange("p g b s -> p b g s"))
                    if j < J - 1:
                        link(ins)
                ins.then_inc(kt_r, 1)
                pool.wait_ge(kt_r, layer + 1)

            def frames():
                pool.memset(V4[:, :, :, :, :], 0.0).then_inc(zero_r, 1)
                pool.memset(VT[:, :, :, :], 0.0).then_inc(zero_r, 1)
                pool.memset(KT[:, :, :, :].bitcast(F32), 0.0).then_inc(zero_r, 1)
                pool.wait_ge(zero_r, 3)
                pool.wait_ge(ones_r, 1)
                pool.wait_ge(small_in, 48)
                for j in range(J):
                    c = 16 * (j % 2) + D
                    for b in range(B):
                        ins = pool.memset(V4[:, b, :, j, c:c + D], 1.0)
                    link(ins)
                    q = slice(32 * j, 32 * j + 32)
                    on = ones[q, :].rearrange("p (b g d) -> p b g d", b=B, g=G)
                    link(pool.tensor_scalar(VT[q, :, :, 16 * j + D:16 * j + 2 * D], on, own[q, 0:1], 1.0,
                                            ALU.mult, ALU.mult))

            def values(layer):
                if layer == 1:
                    pool.wait_ge(pv_r, ROUNDS * B)
                pool.wait_ge(bias_r, 4)
                for t, bias in ((0, rows_sb[:, RV + layer, :]), (1, bvt[:, layer, :])):
                    pool.wait_ge(vf_r, 2 * layer + t + 1)
                    src = vf[:, t, :].rearrange("p (b g j d) -> p b g j d", b=B, g=G, j=J)
                    bias = bias.rearrange("p (g j d) -> p g j d", g=G, j=J)
                    for j in range(J):
                        for b in range(B):
                            if t == 0:
                                ins = pool.tensor_tensor(V4[:, b, :, j, 16 * (j % 2):16 * (j % 2) + D], src[:, b, :, j, :],
                                                         bias[:, :, j, :], ALU.add)
                            else:
                                q = slice(32 * j, 32 * j + 32)
                                ins = pool.tensor_tensor(VT[q, b, :, 16 * j:16 * j + D], src[q, b, :, j, :],
                                                         bias[q, :, j, :], ALU.add)
                                if (b, j) != (B - 1, J - 1):
                                    link(ins)
                    if t == 0:
                        link(ins)
                ins.then_inc(v_r, 1)
                pool.wait_ge(v_r, layer + 1)

            def biased(layer, b):
                n = B * layer + b
                if n >= 2:
                    pool.wait_ge(res_r, n - 1)
                if layer == 1:
                    pool.wait_ge(x2_r, b + 1)
                else:
                    pool.wait_ge(x_in[b], 16)
                pool.wait_ge(bias_r, 4)
                for t in range(TT):
                    ins = pool.tensor_tensor(xg[:, n % 2, t, :], xr[:, TT * b + t, :], bog[:, layer, :], ALU.add)
                ins.then_inc(xg_r, 1)

            def root(k):
                pool.wait_ge(mv_r, k + 1)
                pool.tensor_scalar(var[:, k % 4, :], mv[:, k % 4, :, 1], EPS, 1.0, ALU.add, ALU.mult).then_inc(var_r, 1)
                pool.wait_ge(var_r, k + 1)
                pool.tensor_tensor(rstd[:, k % 4, :], var[:, k % 4, :], half[:, :], ALU.pow).then_inc(rstd_r, 1)

            pool.wait_ge(half_r, 1)
            clear(0)
            for layer in range(2):
                root(norm_no["pre", layer, 0])
                root(norm_no["pre", layer, 1])
                if layer == 0:
                    for n in (1, 2):
                        pool.memset(Q4[n][:, :, :].bitcast(F32), 0.0).then_inc(q4_clear, 1)
                    frames()
                    values(0)
                    tail_keys(0)
                for i in range(-1, B + 1):
                    if 0 <= i + 2 < B and i >= 0:
                        root(norm_no["pre", layer, i + 2])
                        diagonal(layer, i + 2)
                    if 0 <= i - 1 < B:
                        root(norm_no["post", layer, i - 1])
                    if 0 <= i + 1 < B:
                        biased(layer, i + 1)
                if layer == 0:
                    keys_late()
                    values(1)
                    tail_keys(1)
                    clear(1)

        @block.scalar
        def _(act):
            act.dma_start(consts_sb[:, :], consts).then_inc(small_in, 16)
            act.dma_start(cols_sb[:, :], cols).then_inc(small_in, 16)
            act.dma_start(rows_sb[:, :, :], rows.partition_broadcast(P)).then_inc(small_in, 16)
            act.wait_ge(small_in, 48)
            act.activation(tg[:, :], rows_sb[:, RG, 0:4], ACT.Tanh).then_inc(gates, 1)
            act.activation(hcols[:, :], cols_sb[:, :], ACT.Copy, scale=0.5)

            def copy_k(layer):
                for g in range(G):
                    for part in range(2):
                        k = 2 * (G * layer + g) + part
                        act.wait_ge(kmm, k + 1)
                        if k >= 2:
                            act.wait_ge(k4_r, k - 1)
                        col = G * layer + g
                        if layer == 1:
                            act.activation(kf[:, k % 2, :], kbank[k % len(kbank)][:, 0:2 * S], ACT.Identity,
                                           bias=cols_sb[:, BK + col:BK + col + 1]).then_inc(kf_r, 1)
                        act.activation(kh[:, k % 2, :], kbank[k % len(kbank)][:, 0:2 * S], ACT.Identity, bias=lcols[:, col:col + 1],
                                       scale=lowrow).then_inc(kh_r, 1)

            def copy_v(layer):
                for t in range(2):
                    act.wait_ge(vmm, 2 * layer + t + 1)
                    act.activation(vf[:, t, :], pv[t][:, :], ACT.Copy).then_inc(vf_r, 1)

            def diagonal(layer, b):
                n = B * layer + b
                act.wait_ge(k4_r, 8 * layer + 8)
                act.wait_ge(kd_clear, 2 * layer + n % 2 + 1)
                for j in range(J):
                    q = slice(32 * j, 32 * j + 32)
                    ins = act.activation(Kd[n % 2][q, :, j, :], K4[q, :, b, :].bitcast(F32), ACT.Copy, scale=keyrow[q, 0:1])
                ins.then_inc(kd_r, 1)

            def copy_normed(kind, layer, b):
                act.wait_ge(misc_full, use[kind, layer, b] + 1)
                if kind == "pre":
                    if (layer, b) != (0, 0):
                        act.wait_ge(qh_r, B * layer + b)
                    dst = xnT[:, :]
                else:
                    dst = pnT[:, b, :]
                    if layer == 1:
                        act.wait_ge(n16_r, B)
                act.activation(dst, misc[:, :], ACT.Copy).then_inc(xnT_r, 1)

            def copy_q(layer, b):
                n = B * layer + b
                act.wait_ge(misc_full, use["q", layer, b] + 1)
                if n >= 2:
                    act.wait_ge(q_in[(n - 2) % 3], 3 * 16 * ((n - 2) // 3 + 1))
                act.activation(qh[:, n % 2, :], misc[:, :], ACT.Identity,
                               bias=cols_sb[:, BQ + layer:BQ + layer + 1]).then_inc(qh_r, 1)

            def copy_top(layer, b):
                n = B * layer + b
                act.wait_ge(misc_full, use["top", layer, b] + 1)
                if n >= 2:
                    act.wait_ge(m_in[(n - 2) % 3], 2 * 16 * ((n - 2) // 3 + 1))
                act.activation(nmT[:, n % 2, :], misc[0:32, :], ACT.Copy).then_inc(nmT_r, 1)

            def exps(layer, b, t):
                k = TILES * (B * layer + b) + t
                act.wait_ge(score_r, k + 1)
                if k >= PRING:
                    m, old = divmod(k - PRING, TILES)
                    act.wait_ge(pv_r, ROUNDS * m + (old // 4 + 1 if old < H else ROUNDS))
                q0 = P if layer == 1 and t >= H else 0
                act.activation(pr[:, k % PRING, q0:T], score[k % SRING][:, q0:T], ACT.Exp, scale=SCALE).then_inc(exp_r, 1)

            def gate_of(b, k):
                act.wait_ge(gmm, 3 * b + k + 1)
                if b > 0:
                    act.wait_ge(c_r, b + 2)
                bias = (hcols[:, BF:BF + 1], hcols[:, BI:BI + 1], cols_sb[:, BC:BC + 1])[k]
                act.activation(gt[:, k, :], top[k][:, :], ACT.Tanh, bias=bias, scale=(0.5, 0.5, 1.0)[k]).then_inc(gt_r, 1)

            copy_normed("pre", 0, 0)
            copy_q(0, 0)
            act.wait_ge(lcol_r, 1)
            copy_k(0)
            for layer in range(2):
                if layer == 1:
                    diagonal(1, 0)
                    diagonal(1, 1)
                    for b in range(ahead(1)):
                        copy_normed("pre", 1, b)
                        copy_q(1, b)
                if layer == 0:
                    diagonal(0, 0)
                    copy_v(0)
                    diagonal(0, 1)
                    act.activation(identr[:, :], ident[:, :], ACT.Copy).then_inc(const_r, 1)
                    act.wait_ge(mask_in, 16)
                    act.activation(maskr[:, :], cmask[:, :], ACT.Copy).then_inc(const_r, 1)
                for i in range(-1, B + 1):
                    for slot in range(SLOTS):
                        if 0 <= i < B and slot < TILES:
                            exps(layer, i, slot)
                        for what, b in planned(ACT_PLAN, layer, i, slot):
                            if what in ("pre", "post"):
                                copy_normed(what, layer, b)
                            elif what == "q":
                                copy_q(layer, b)
                            elif what == "top":
                                copy_top(layer, b)
                            else:
                                gate_of(b, int(what[4]))
                        if (layer, i, slot) == WEIGHTS_AT:
                            for k in range(3):
                                n = min(4, 9 - 4 * k)
                                act.wait_ge(misc_full, use["w", k] + 1)
                                act.activation(wfT[:, 4 * k:4 * k + n, :], misc[:, 0:n * P], ACT.Copy).then_inc(wT_r, 1)
                if layer == 0:
                    def up16(c):
                        act.wait_ge(sc_r, 2)
                        act.activation(u16[:, c, :, :], uf[:, c, :, :], ACT.Copy, scale=sc[:, 1, 2:3]).then_inc(u16_r, 1)

                    for t in range(24):
                        act.wait_ge(fmm, t + 1)
                        dst = uf if t < 12 else gf
                        act.activation(dst[:, t % 12 // 3, t % 3, :], fbank[t % FRING][:, :], ACT.Copy).then_inc(fev, 1)
                        if t in (19, 21):
                            up16((t - 19) // 2)
                    up16(2)
                    up16(3)
                    for c in range(B):
                        act.wait_ge(g16_r, c + 1)
                        act.wait_ge(sc_r, 3)
                        act.activation(gf[:, c, :, :], g16[:, c, :, :], ACT.Tanh, scale=sc[:, 2, 3:4]).then_inc(th_r, 1)
                        if c > 0:
                            act.wait_ge(th_r, c + 1)
                            act.activation(s16[:, c, :, :], gf[:, c, :, :], ACT.Copy, bias=32768.0, scale=32768.0)\
                               .then_inc(s16a_r, 1)
                    copy_k(1)
                    copy_v(1)
                    for c in range(1, B):
                        act.wait_ge(sc_r, 4)
                        act.activation(g16[:, c, :, :], gf[:, c, :, :], ACT.Copy, scale=sc[:, 3, 3:4]).then_inc(n2a_r, 1)
                    for c in range(1, B):
                        act.wait_ge(n3_r, c + 1)
                        act.activation(gf[:, c, :, :], g16[:, c, :, :], ACT.Copy, scale=sc[:, 4, 1:2]).then_inc(xo_r, 1)
            for b in range(B):
                act.wait_ge(ymm, b + 1)
                act.activation(yt[:, b, :, :], ybank[b][:, :], ACT.Tanh).then_inc(y_r, 1)

        @block.tensor
        def _(pe):
            def keys(layer):
                if layer == 1:
                    pe.wait_ge(wl_in, 32)
                for g in range(G):
                    for part in range(2):
                        k = 2 * (G * layer + g) + part
                        if k >= len(kbank):
                            pe.wait_ge(k4_r if layer == 0 else kh_r, k - len(kbank) + 1)
                        pe.matmul(kbank[k % len(kbank)][:, 0:2 * S], wkr_sb[:, layer, g, :],
                                  ctx_sb[:, 2 * part:2 * part + 2, :], start=True, stop=True).then_inc(kmm, 1)

            def values(layer):
                pe.wait_ge(tail_in, 16)
                pe.wait_ge(*((w_in, 16) if layer == 0 else (wl_in, 32)))
                for t in range(2):
                    for b in range(B):
                        keys = (ctx_sb[:, b, 0:P], tail_sb[:, b, :])[t]
                        ins = pe.matmul(pv[t][:, P * b:P * b + P], keys, weight(WL1 * layer + WV), start=True, stop=True)
                    ins.then_inc(vmm, 1)

            def turn_normed(kind, layer, b):
                k = norm_no[kind, layer, b]
                pe.wait_ge(xn_r, k + 1)
                fill_misc(pe, (kind, layer, b))
                for t in range(TT):
                    ins = pe.transpose(misc[:, P * t:P * t + P], xn[:, kind == "post", t, :], ident[:, :])
                ins.then_inc(misc_full, 1)

            def project_q(layer, b):
                pe.wait_ge(xnT_r, norm_no["pre", layer, b] + 1)
                fill_misc(pe, ("q", layer, b))
                pe.matmul(misc[:, :], weight(WL1 * layer + WQ), xnT[:, :], start=True, stop=True).then_inc(misc_full, 1)

            def scores_for_top(layer, b, u):
                n = B * layer + b
                k = units_before(n) + u
                if u == 0:
                    pe.wait_ge(q_in[n % 3], 3 * 16 * (n // 3 + 1))
                    pe.wait_ge(kd_r, n + 1)
                if k >= MRING:
                    pe.wait_ge(top_red, k - MRING + 1)
                qt, h0, heads, keys = UNITS[layer][u]
                masked = layer == 1 and qt < 2
                ps = top[k % MRING]
                g, j = h0 // J, h0 % J
                cols = ps[:, 0:keys * heads].rearrange("p (h k) -> p h k", h=heads)
                ins = pe.matmul(cols, Q4[n % 3][:, g, P * qt:P * qt + P], Kd[n % 2][:, g, j:j + heads, 0:keys],
                                start=True, stop=not masked, skip_group_check=True)
                if masked:
                    lo = 0 if qt == 0 else P
                    ins = pe.matmul(cols[:, :, lo:keys], identr[:, :],
                                    maskM[:, 0:keys - lo].unsqueeze(1).to_broadcast([P, heads, keys - lo]),
                                    start=False, stop=True, skip_group_check=True)
                ins.then_inc(top_r, 1)

            def turn_top(layer, b):
                n = B * layer + b
                pe.wait_ge(nms_r, n + 1)
                fill_misc(pe, ("top", layer, b))
                for t in range(TT):
                    ins = pe.transpose(misc[0:32, P * t:P * t + P],
                                       nms[:, t, :, :, :].rearrange("p a j g -> p (a j g)").bitcast(F32), ident[:, :])
                ins.then_inc(misc_full, 1)

            def scores(layer, b, t):
                n = B * layer + b
                k = TILES * n + t
                if t == 0:
                    pe.wait_ge(m_in[n % 3], 2 * 16 * (n // 3 + 1))
                if k >= SRING:
                    pe.wait_ge(exp_r, k - SRING + 1)
                ps = score[k % SRING]
                if t < H:
                    g, j = t % G, t // G
                    ins = pe.matmul(ps[:, :], K4[32 * j:32 * j + 32, g, b, 0:P],
                                    Q4[n % 3][32 * j:32 * j + 32, g, :], start=True, stop=(layer == 0),
                                    skip_group_check=True)
                    if layer == 1:
                        ins = pe.matmul(ps[:, 0:P], identr[:, :], maskT, start=False, stop=True, skip_group_check=True)
                else:
                    if t == H and b == 0:
                        pe.wait_ge(kt_r, layer + 1)
                    q0 = P if layer == 1 else 0
                    ins = pe.matmul(ps[:, q0:T], KT[:, b, t - H, :], Q4[n % 3][:, t - H, q0:T],
                                    start=True, stop=(layer == 0), skip_group_check=True)
                    if layer == 1:
                        ins = pe.matmul(ps[:, P:P + 32], identr[:, :], maskE, start=False, stop=True,
                                        skip_group_check=True)
                ins.then_inc(score_r, 1)

            def weigh(layer, b, r):
                n = B * layer + b
                if r == 0 and b == 0:
                    pe.wait_ge(v_r, layer + 1)
                if r in (0, 2) and n > 0:
                    pe.wait_ge(pvx, 2 * (n - 1) + r // 2 + 1)
                pe.wait_ge(exp_r, TILES * n + (4 * r + 4 if r < 4 else TILES))
                acc = pv[r // 2 if r < 4 else r - 4]
                q0 = P if layer == 1 and r >= 4 else 0
                for g in range(G):
                    if r < 4:
                        lhs, t = V4[:, b, g, r, :], 4 * r + g
                    else:
                        lhs, t = VT[:, b, g, 32 * (r - 4):32 * (r - 4) + 32], H + g
                    ins = pe.matmul(acc[32 * g:32 * g + 32, q0:T], lhs, pr[:, (TILES * n + t) % PRING, q0:T],
                                    start=(r in (0, 2)), stop=(r >= 4), skip_group_check=True)
                ins.then_inc(pv_r, 1)

            def project_out(layer, b):
                n = B * layer + b
                pe.wait_ge(oT_r, n + 1)
                fill_misc(pe, ("wo", layer, b))
                for t in range(TT):
                    ins = pe.matmul(misc[:, P * t:P * t + P], oT[:, P * t:P * t + P], weight(WL1 * layer + WO),
                                    start=True, stop=True)
                ins.then_inc(misc_full, 1)

            def state(b, k):
                if k == 0:
                    pe.wait_ge(c_r, b + 2)
                    pe.wait_ge(top_red, units_before(2 * B))
                if b > 0:
                    pe.wait_ge(gt_r, 3 * b - 2 + k)
                pe.matmul(top[k][:, :], weight((UF, UI, UC)[k]), cst[:, :], start=True, stop=False, skip_group_check=True)

            def step(b, k):
                if k == 0:
                    pe.wait_ge(xnT_r, norm_no["post", 1, b] + 1)
                pe.matmul(top[k][:, :], weight((WF, WI, WC)[k]), pnT[:, b, :], start=False, stop=True,
                          skip_group_check=True).then_inc(gmm, 1)

            def outputs_x(b):
                if b == 0:
                    pe.wait_ge(bfo_r, 3)
                    pe.wait_ge(exp_r, 2 * TILES * B)
                if b == 2:
                    pe.wait_ge(pvx, 2 * 2 * B)
                for a in range(2):
                    pe.matmul(ybank[b][:, :], onesr[:, :], bfo[:, a:a + 1, :].to_broadcast([1, TT, C]),
                              start=(a == 0), stop=False, skip_group_check=True)
                for t in range(TT):
                    pe.matmul(ybank[b][:, P * t:P * t + P], pnT[:, b, P * t:P * t + P], weight(WOUT),
                              start=False, stop=False, skip_group_check=True)

            def turn_weights():
                pe.wait_ge(wq_r, 1)
                for k in range(3):
                    fill_misc(pe, ("w", k))
                    for m in range(4 * k, min(4 * k + 4, 9)):
                        blk = wf_sb[:, 4 * m:4 * m + 4, :].rearrange("p a c -> p (a c)")
                        ins = pe.transpose(misc[:, P * (m % 4):P * (m % 4) + P], blk, ident[:, :])
                    ins.then_inc(misc_full, 1)

            def global_top(k):
                pe.wait_ge(amx_r, k + 1)
                fill_misc(pe, ("gt", k))
                pe.transpose(misc[0:1, 0:P], amx[:, k:k + 1], ident[:, :]).then_inc(misc_full, 1)
                pe.wait_ge(gtop_r, k + 1)
                fill_misc(pe, ("gb", k))
                pe.matmul(misc[:, 0:1], ones[0:1, :], gtop[0:1, k:k + 1], start=True, stop=True).then_inc(misc_full, 1)

            pe.wait_ge(small_in, 48)
            turn_normed("pre", 0, 0)
            pe.wait_ge(w_in, 16)
            project_q(0, 0)
            pe.wait_ge(k_in, 32)
            keys(0)
            values(0)
            for layer in range(2):
                for i in range(-1, B + 1):
                    for slot in range(SLOTS):
                        if 0 <= i < B and slot < TILES:
                            scores(layer, i, slot)
                        for b, u in units_at(layer, i, slot):
                            scores_for_top(layer, b, u)
                        for what, b in planned(PE_PLAN, layer, i, slot):
                            if what in ("pre", "post"):
                                turn_normed(what, layer, b)
                            elif what == "q":
                                project_q(layer, b)
                            elif what == "top":
                                turn_top(layer, b)
                            elif what == "wo":
                                project_out(layer, b)
                            elif what.startswith("round"):
                                weigh(layer, b, int(what[5]))
                            elif what.startswith("tail"):
                                weigh(layer, b, 4 + int(what[4]))
                            elif what.startswith("state"):
                                state(b, int(what[5]))
                            else:
                                step(b, int(what[4]))
                        if (layer, i) == (1, B) and slot in (3, 4, 9):
                            outputs_x((3, 4, 9).index(slot))
                        if (layer, i, slot) == WEIGHTS_AT:
                            turn_weights()
                if layer == 0:
                    pe.wait_ge(ones_r, 1)
                    pe.wait_ge(wT_r, 3)
                    pe.wait_ge(pvx, 2 * B)
                    pe.wait_ge(exp_r, TILES * B)
                    pe.wait_ge(top_red, units_before(B))
                    global_top(0)
                    for t in range(24):
                        c, m = t % 12 // 3, t % 3
                        if t < 12 and m == 0:
                            pe.wait_ge(xq_r, c + 1)
                        if t >= FRING:
                            pe.wait_ge(fev, t - FRING + 1)
                        pe.matmul(fbank[t % FRING][:, :], wfT[:, 3 * (1 - t // 12) + m, :], xq[:, c, :],
                                  start=True, stop=True).then_inc(fmm, 1)
                        if t == 14:
                            global_top(1)
                    for k in range(2, 5):
                        if k == 3:
                            pe.wait_ge(fev, 24)
                            keys(1)
                            values(1)
                        global_top(k)
                    for c in range(B):
                        pe.wait_ge(*((xo_r, c) if c > 0 else (xod_r, 1)))
                        if c == 0:
                            pe.wait_ge(kh_r, 4 * G)
                        for t in range(TT):
                            for m in range(NF):
                                ins = pe.matmul(fbank[c][:, P * t:P * t + P], gf[:, c, m, P * t:P * t + P],
                                                wfT[:, 6 + m, :], start=(t == 0 and m == 0), stop=(m == NF - 1),
                                                skip_group_check=True)
                        ins.then_inc(dmm, 1)
                        if c == 2:
                            turn_normed("pre", 1, 0)
                    project_q(1, 0)
                    turn_normed("pre", 1, 1)
                    project_q(1, 1)
                    pe.wait_ge(x2_r, B)
                    pe.wait_ge(const_r, 2)
            outputs_x(B - 1)
            pe.wait_ge(c_r, B + 2)
            for b in range(B):
                for t in range(TT):
                    ins = pe.matmul(ybank[b][:, P * t:P * t + P], cst[:, P * t:P * t + P], weight(UOUT),
                                    start=False, stop=True, skip_group_check=True)
                ins.then_inc(ymm, 1)

        @block.vector
        def _(dve):
            chained = [0]
            chain = ctx.enter_context(nc.semaphore("chain"))

            def link(ins):
                chained[0] += 1
                ins.then_inc(chain, 1)
                dve.wait_ge(chain, chained[0])

            def keys():
                for g in range(G):
                    for part in range(2):
                        k = 2 * g + part
                        dve.wait_ge(kh_r, k + 1)
                        dst = K4[:, g, 2 * part:2 * part + 2, :].rearrange("p b s -> p (b s)")
                        dve.scalar_tensor_tensor(out=dst, in0=kbank[k % len(kbank)][:, 0:2 * S],
                                                 scalar=cols_sb[:, BK + g:BK + g + 1],
                                                 in1=kh[:, k % 2, :].bitcast(F32), op0=ALU.add,
                                                 op1=ALU.subtract).then_inc(k4_r, 1)

            def weights():
                dve.wait_ge(wf_in, 16)
                link(dve.tensor_reduce(wabs[:, 0, :], wf_sb[:, :, :], AX.X, ALU.max, apply_absolute_value=True))
                link(dve.tensor_scalar(wabs[:, 1, :], wabs[:, 0, :], 1.0 / WMAX, SMIN, ALU.mult, ALU.max))
                link(dve.reciprocal(wabs[:, 2, :], wabs[:, 1, :]))
                wide = [P, NBLK, 32]
                link(dve.tensor_tensor(wn16[:, :, :], wf_sb[:, :, :],
                                       wabs[:, 2, :].unsqueeze(2).to_broadcast(wide), ALU.mult))
                link(dve.tensor_scalar(wn16[:, :, :], wn16[:, :, :], WMAX, -WMAX - 1.0, ALU.min, ALU.max))
                dve.tensor_tensor(wf_sb[:, :, :], wn16[:, :, :],
                                  wabs[:, 1, :].unsqueeze(2).to_broadcast(wide), ALU.mult).then_inc(wq_r, 1)

            def norm_stats(kind, layer, b):
                k = norm_no[kind, layer, b]
                if (kind, layer) == ("pre", 0):
                    dve.wait_ge(x_in[b], 16)
                elif kind == "pre":
                    dve.wait_ge(x2_r, b + 1)
                else:
                    dve.wait_ge(res_r, B * layer + b + 1)
                for t in range(TT):
                    ins = dve.bn_stats(stat6[:, k % 4, t, :], xr[:, TT * b + t, :])
                link(ins)
                for t in range(TT):
                    ins = dve.bn_aggr(mv[:, k % 4, t, :], stat6[:, k % 4, t, :])
                ins.then_inc(mv_r, 1)

            def norm(kind, layer, b):
                k = norm_no[kind, layer, b]
                dve.wait_ge(mv_r, k + 1)
                dve.wait_ge(rstd_r, k + 1)
                if B * layer + b > 0:
                    dve.wait_ge(xnT_r, norm_no[kind, (B * layer + b - 1) // B, (b - 1) % B] + 1)
                for t in range(TT):
                    ins = dve.tensor_scalar(xn[:, kind == "post", t, :], xr[:, TT * b + t, :], mv[:, k % 4, t, 0:1],
                                            rstd[:, k % 4, t:t + 1], ALU.subtract, ALU.mult)
                ins.then_inc(xn_r, 1)

            def normed_max(b):
                dve.wait_ge(xn_r, norm_no["post", 0, b] + 1)
                dve.tensor_reduce(amax[:, 0, b:b + 1], xn[:, 1, :, :], AX.XY, ALU.max,
                                  apply_absolute_value=True).then_inc(am_r, 1)

            def q_low(layer, b):
                n = B * layer + b
                dve.wait_ge(qh_r, n + 1)
                if n >= 2:
                    dve.wait_ge(q_in[(n - 2) % 3], 3 * 16 * ((n - 2) // 3 + 1))
                dve.scalar_tensor_tensor(out=ql[:, n % 2, :], in0=misc[:, :],
                                         scalar=cols_sb[:, BQ + layer:BQ + layer + 1],
                                         in1=qh[:, n % 2, :].bitcast(F32), op0=ALU.add,
                                         op1=ALU.subtract).then_inc(ql_r, 1)

            def take_top(layer, b, u):
                k = units_before(B * layer + b) + u
                qt, h0, heads, keys = UNITS[layer][u]
                dve.wait_ge(top_r, k + 1)
                dve.tensor_reduce(nm[:, qt, h0:h0 + heads],
                                  top[k % MRING][:, 0:keys * heads].rearrange("p (h k) -> p h k", h=heads),
                                  AX.X, ALU.max, negate=True).then_inc(top_red, 1)

            def split_top(layer, b):
                n = B * layer + b
                dve.wait_ge(top_red, units_before(n + 1))
                src = nm[:, :, :].rearrange("p t (g j) -> p t j g", g=G)
                part = [nms[:, :, a, :, :] for a in range(2)]
                if n > 0:
                    dve.wait_ge(nmT_r, n)
                dve.tensor_copy(part[0], src).then_inc(nmh_r, 1)
                dve.wait_ge(nmh_r, n + 1)
                dve.tensor_tensor(part[1], src, part[0].bitcast(F32), ALU.subtract).then_inc(nms_r, 1)

            def divide(layer, b, part):
                n = B * layer + b
                if part < 2:
                    dve.wait_ge(pv_r, ROUNDS * n + 5 + part)
                    dve.transpose(oq[:, part, :, :, :].rearrange("p k e r -> p (k e r)"), pv[part][:, :]).then_inc(pvx, 1)
                elif part == 2:
                    dve.wait_ge(pvx, 2 * n + 2)
                    link(dve.reciprocal(orc[:, :, :, :].rearrange("p a k e -> p (a k) e"),
                                        oq[:, :, :, :, D].rearrange("p a k e -> p (a k) e")))
                    for a in range(2):
                        ins = dve.tensor_tensor(oc[:, :, a, :, :], oq[:, a, :, :, 0:D],
                                                orc[:, a, :, :].unsqueeze(3).to_broadcast([P, T // 32, 2, D]), ALU.mult)
                    ins.then_inc(oc_r, 1)
                else:
                    dve.wait_ge(oc_r, n + 1)
                    if n > 0:
                        dve.wait_ge(misc_full, use["wo", (n - 1) // B, (n - 1) % B] + 1)
                    dve.transpose(oT[:, :], oc[:, :, :, :, :].rearrange("p k a e d -> p (k a e d)")).then_inc(oT_r, 1)

            def residual(layer, b):
                n = B * layer + b
                dve.wait_ge(misc_full, use["wo", layer, b] + 1)
                dve.wait_ge(xg_r, n + 1)
                dve.scalar_tensor_tensor(out=xr[:, TT * b:TT * b + TT, :].rearrange("p t c -> p (t c)"),
                                         in0=misc[:, :], scalar=tg[:, layer:layer + 1],
                                         in1=xg[:, n % 2, :, :].rearrange("p t c -> p (t c)"),
                                         op0=ALU.mult, op1=ALU.add).then_inc(res_r, 1)

            def update(b):
                if b == 0:
                    dve.wait_ge(v_r, 2)
                dve.wait_ge(gt_r, 3 * b + 1)
                dve.scalar_tensor_tensor(out=tmp[:, 0, :], in0=gt[:, 0, :], scalar=1.0, in1=cst[:, :],
                                         op0=ALU.add, op1=ALU.mult).then_inc(ct_r, 1)
                dve.wait_ge(gt_r, 3 * b + 3)
                dve.scalar_tensor_tensor(out=tmp[:, 1, :], in0=gt[:, 1, :], scalar=1.0, in1=gt[:, 2, :],
                                         op0=ALU.add, op1=ALU.mult).then_inc(ct_r, 1)
                dve.wait_ge(ct_r, 2 * b + 2)
                dve.scalar_tensor_tensor(out=cst[:, :], in0=tmp[:, 0, :], scalar=0.5, in1=tmp[:, 1, :],
                                         op0=ALU.mult, op1=ALU.add).then_inc(c_r, 1)

            def part_max(k, n_parts):
                dve.wait_ge(am_r, am_count[k])
                dve.tensor_reduce(amx[:, k:k + 1], amax[:, k, 0:n_parts], AX.X, ALU.max).then_inc(amx_r, 1)

            def full_max(k):
                dve.wait_ge(misc_full, use["gt", k] + 1)
                dve.tensor_reduce(gtop[0:1, k:k + 1], misc[0:1, 0:P], AX.X, ALU.max).then_inc(gtop_r, 1)

            def factors(src, to, constant, aps):
                while True:
                    first, second = constant, aps[0] if aps else None
                    constant, aps = (aps[1] if len(aps) > 1 else None), aps[2:]
                    ins = dve.tensor_scalar(to, src, first, second, ALU.mult, *((ALU.mult,) if second is not None else ()))
                    if constant is None:
                        return ins
                    link(ins)
                    src = to

            def scale_of(k, raw=1.0, aps=()):
                dve.wait_ge(gtop_r, k + 1)
                dve.wait_ge(misc_full, use["gb", k] + 1)
                factors(misc[:, 0:1], sc[:, k, 0:1], raw, aps).then_inc(smax_r, 1)
                dve.wait_ge(smax_r, k + 1)
                link(dve.tensor_scalar(sc[:, k, 1:2], sc[:, k, 0:1], 1.0 / QMAX, SMIN, ALU.mult, ALU.max))
                link(dve.reciprocal(sc[:, k, 2:3], sc[:, k, 1:2]))
                src, constant = (sc[:, k, 1:2], 0.5) if k == 2 else (sc[:, k, 2:3], raw)
                factors(src, sc[:, k, 3:4], constant, aps).then_inc(sc_r, 1)
                dve.wait_ge(sc_r, k + 1)

            def ffn():
                flat = lambda t, c: t[:, c, :, :].rearrange("p m t -> p (m t)")

                def whole_max(k, c, src):
                    dve.tensor_reduce(amax[:, k, c:c + 1], flat(src, c), AX.X, ALU.max,
                                      apply_absolute_value=True).then_inc(am_r, 1)

                def absmax(k, t, src):
                    dve.wait_ge(fev, t + 1)
                    dve.tensor_reduce(amax[:, k, t % 12:t % 12 + 1], src[:, t % 12 // 3, t % 3, :], AX.X, ALU.max,
                                      apply_absolute_value=True).then_inc(am_r, 1)

                part_max(0, B)
                full_max(0)
                scale_of(0)
                for c in range(B):
                    dve.wait_ge(xnT_r, norm_no["post", 0, B - 1] + 1)
                    dve.tensor_scalar(n16[:, c, :], pnT[:, c, :], sc[:, 0, 2:3], None, ALU.mult).then_inc(n16_r, 1)
                    dve.wait_ge(n16_r, c + 1)
                    dve.tensor_scalar(xq[:, c, :], n16[:, c, :], sc[:, 0, 1:2], None, ALU.mult).then_inc(xq_r, 1)

                for t in range(24):
                    absmax(1 + t // 12, t, uf if t < 12 else gf)
                    if t == 11:
                        part_max(1, 12)
                    if t == 13:
                        full_max(1)
                    if t == 15:
                        scale_of(1)
                part_max(2, 12)
                full_max(2)
                scale_of(2)
                for c in range(B):
                    dve.tensor_scalar(flat(g16, c), flat(gf, c), sc[:, 2, 2:3], None, ALU.mult).then_inc(g16_r, 1)
                for c in range(B):
                    dve.wait_ge(th_r, c + 1)
                    if c == 0:
                        dve.tensor_scalar(flat(s16, c), flat(gf, c), 32768.0, 32768.0, ALU.mult, ALU.add).then_inc(s16_r, 1)
                        dve.wait_ge(s16_r, 1)
                    else:
                        dve.wait_ge(s16a_r, c)
                    dve.wait_ge(g16_r, c + 1)
                    dve.tensor_tensor(flat(gf, c), flat(g16, c), flat(s16, c), ALU.mult).then_inc(g2_r, 1)
                    dve.wait_ge(g2_r, c + 1)
                    whole_max(3, c, gf)
                part_max(3, B)
                full_max(3)
                scale_of(3, 2.0 ** -16, (sc[:, 2, 1:2],))
                for c in range(B):
                    if c == 0:
                        dve.tensor_scalar(flat(g16, c), flat(gf, c), sc[:, 3, 3:4], None, ALU.mult).then_inc(n2_r, 1)
                        dve.wait_ge(n2_r, 1)
                    else:
                        dve.wait_ge(n2a_r, c)
                    dve.wait_ge(u16_r, c + 1)
                    dve.tensor_tensor(flat(uf, c), flat(g16, c), flat(u16, c), ALU.mult).then_inc(o_r, 1)
                    dve.wait_ge(o_r, c + 1)
                    whole_max(4, c, uf)
                part_max(4, B)
                full_max(4)
                scale_of(4, 1.0, (sc[:, 3, 1:2], sc[:, 1, 1:2]))
                for c in range(B):
                    dve.tensor_scalar(flat(g16, c), flat(uf, c), sc[:, 4, 3:4], None, ALU.mult).then_inc(n3_r, 1)
                    if c == 0:
                        dve.wait_ge(n3_r, 1)
                        dve.tensor_scalar(flat(gf, c), flat(g16, c), sc[:, 4, 1:2], None, ALU.mult).then_inc(xod_r, 1)
                for c in range(B):
                    dve.wait_ge(dmm, c + 1)
                    xc = xr[:, TT * c:TT * c + TT, :].rearrange("p t c -> p (t c)")
                    dve.scalar_tensor_tensor(out=xc, in0=fbank[c][:, :], scalar=tg[:, 2:3], in1=xc,
                                             op0=ALU.mult, op1=ALU.add).then_inc(x2_r, 1)
                    if c < ahead(1):
                        norm_stats("pre", 1, c)
                        norm("pre", 1, c)
                    if c == 2:
                        q_low(1, 0)
                q_low(1, 1)

            am_count = {0: 4, 1: 16, 2: 28, 3: 32, 4: 36}

            dve.memset(ones[:, :], 1.0).then_inc(ones_r, 1)
            dve.memset(Q4[0][:, :, :].bitcast(F32), 0.0).then_inc(q4_clear, 1)
            dve.wait_ge(ones_r, 1)
            norm_stats("pre", 0, 0)
            norm("pre", 0, 0)
            dve.wait_ge(small_in, 48)
            dve.tensor_scalar(lcols[:, :], cols_sb[:, BK:BK + 2 * G], lowrow, None, ALU.mult).then_inc(lcol_r, 1)
            dve.wait_ge(gates, 1)
            for n in range(2):
                dve.tensor_scalar(bog[:, n, :], rows_sb[:, RO + n, :], tg[:, n:n + 1], None, ALU.mult).then_inc(bias_r, 1)
            for n in range(2):
                dve.tensor_scalar(bvt[:, n, :], rows_sb[:, RV + n, :], own[:, 0:1], None, ALU.mult).then_inc(bias_r, 1)
            dve.tensor_copy(onesr[:, :], ones[0:1, :]).then_inc(bfo_r, 1)
            dve.tensor_copy(bfo[:, 0, :], rows_sb[0:1, RFO, :]).then_inc(bfo_r, 1)
            dve.wait_ge(bfo_r, 2)
            dve.tensor_tensor(bfo[:, 1, :], rows_sb[0:1, RFO, :], bfo[:, 0, :].bitcast(F32), ALU.subtract).then_inc(bfo_r, 1)
            norm_stats("pre", 0, 1)
            q_low(0, 0)
            keys()

            for layer in range(2):
                for i in range(-1, B + 1):
                    for slot in range(SLOTS):
                        for b, u in units_at(layer, i, slot):
                            take_top(layer, b, u)
                        for what, b in planned(DVE_PLAN, layer, i, slot):
                            if what.startswith("stat"):
                                if (what, b) != ("stat pre", 1):
                                    norm_stats(what[5:], layer, b)
                            elif what.startswith("div"):
                                divide(layer, b, int(what[3]))
                            elif what == "wo":
                                residual(layer, b)
                            elif what in ("pre", "post"):
                                norm(what, layer, b)
                            elif what == "amax":
                                normed_max(b)
                            elif what == "q":
                                q_low(layer, b)
                            elif what == "top":
                                split_top(layer, b)
                            else:
                                update(b)
                        if layer == 0 and i == B - 1 and slot == 16:
                            weights()
                    if layer == 0 and i == B - 1:
                        dve.tensor_scalar(cst[:, :].rearrange("p (t c) -> p t c", c=P),
                                          ones[:, :].unsqueeze(1).to_broadcast([P, TT, P]),
                                          cols_sb[:, INC:INC + 1], 2.0, ALU.mult, ALU.mult).then_inc(c_r, 1)
                        dve.wait_ge(wl_in, 32)
                        for wu in (UF, UI, UC, UOUT):
                            ins = dve.tensor_scalar(wsb[:, wu, :], wsb[:, wu, :], 0.5, None, ALU.mult)
                        ins.then_inc(c_r, 1)
                if layer == 0:
                    ffn()
            for b in range(B):
                dve.wait_ge(y_r, b + 1)
                yb = yt[:, b, :, :].rearrange("p t c -> p (t c)")
                xb = xr[:, TT * b:TT * b + TT, :].rearrange("p t c -> p (t c)")
                dve.scalar_tensor_tensor(out=xb, in0=yb, scalar=tg[:, 3:4], in1=xb,
                                         op0=ALU.mult, op1=ALU.add).then_inc(out_r, 1)


_WEIGHTS = ["L0_xattn_Wq", "L0_xattn_Wv", "L0_xattn_Wo", "L1_xattn_Wq", "L1_xattn_Wv", "L1_xattn_Wo",
            "L1_ffn_wf", "L1_ffn_uf", "L1_ffn_wi", "L1_ffn_ui", "L1_ffn_wc", "L1_ffn_uc", "L1_ffn_wo",
            "L1_ffn_uo"]


def constants():
    a = np.arange(P)
    ident = np.eye(P)
    top = np.where(a[None, :] > a[:, None], NEG, 0.0)
    main = np.where(a[:, None] > a[None, :], NEG, 0.0)
    tail = np.where((a % 32)[:, None] > np.arange(32)[None, :] + OWN, NEG, 0.0)
    own = (a % 32 >= OWN)[:, None]
    low = (a % PARTS == 2)[:, None]
    key = (a % PARTS < 3)[:, None]
    return tuple(np.concatenate(parts, axis=1).astype(np.float32) for parts in ((ident, own, low, key), (top, main, tail)))


def kernel(**inputs):
    import concourse.bacc as bacc
    from concourse.bass_utils import run_bass_kernel_spmd

    order = np.arange(C).reshape(G, J, D).transpose(1, 2, 0).reshape(-1)
    turned = []
    for name in _WEIGHTS:
        t = np.asarray(inputs[name]).T
        turned.append(t[:, order] if name.endswith("Wq") else t)
    wkr = np.zeros((C, 2, G, J, 32), np.float32)
    bkr = np.ones((J, 32, 2, G), np.float32)
    for n in range(2):
        wk = np.asarray(inputs[f"L{n}_xattn_Wk"]).T.reshape(C, G, J, D)
        bk = np.asarray(inputs[f"L{n}_xattn_bk"]).reshape(G, J, D)
        for part in range(3):
            wkr[:, n, :, :, part::PARTS] = wk
            bkr[:, part::PARTS, n, :] = bk.transpose(1, 2, 0)
    ctx = np.asarray(inputs["ctx_1024"]).transpose(2, 0, 1)
    tail = np.zeros((C, B, 4, 32), np.float32)
    tail[:, :, :, OWN:] = ctx[:, :, None, P:]
    wffn = [np.asarray(inputs[f"L0_ffn_w_{n}"]).reshape(NF, P, C).transpose(1, 0, 2).reshape(P, -1) for n in ("gate", "up")]
    wffn.append(np.asarray(inputs["L0_ffn_w_down"]))
    cols = [np.asarray(inputs[f"{n}"])[order] for n in ("L0_xattn_bq", "L1_xattn_bq")]
    cols += [np.asarray(inputs[f"L1_ffn_{n}"]) for n in ("bf", "bi", "bc", "in_c")]
    gates = np.zeros(C, np.float32)
    gates[0:2], gates[2:4] = inputs["g_xattn"], inputs["g_ffn"]
    rows = [np.asarray(inputs[n]) for n in ("L0_xattn_bv", "L1_xattn_bv", "L0_xattn_bo", "L1_xattn_bo", "L1_ffn_bo")]
    arrays = {
        "x": np.asarray(inputs["x"]),
        "w": np.stack(turned, axis=1),
        "wkr": wkr.reshape(C, 2, G, P),
        "ctxT": ctx,
        "tailT": tail.reshape(C, B, P),
        "wffn": np.concatenate(wffn, axis=1).reshape(P, NBLK, 32),
        "cols": np.concatenate([np.stack(cols, axis=1), bkr.reshape(P, 2 * G)], axis=1),
        "rows": np.stack(rows + [gates], axis=0),
        "consts": constants()[0],
        "masks": constants()[1],
    }
    arrays = {k: np.ascontiguousarray(v) for k, v in arrays.items()}
    nc = bacc.Bacc("TRN2", target_bir_lowering=False, num_devices=1)
    args = [nc.dram_tensor(k, v.shape, F32, kind="ExternalInput").ap() for k, v in arrays.items()]
    out = nc.dram_tensor("out", (B, T, C), F32, kind="ExternalOutput").ap()
    program(nc, *args, out)
    result = run_bass_kernel_spmd(nc, [arrays], core_ids=[0])
    return result.results[0]["out"]
```
